# Optimizing a Trainium2 kernel written in Bass

```python
import numpy as np
import jax
import jax.numpy as jnp

def _softmax(x, axis=-1):
    return jax.nn.softmax(x, axis=axis)

def _gelu(x):
    return jax.nn.gelu(x, approximate=True)

def _silu(x):
    return jax.nn.silu(x)

def _sigmoid(x):
    return jax.nn.sigmoid(x)

def _layernorm(x, axis=-1, eps=1e-05):
    m = jnp.mean(x, axis=axis, keepdims=True)
    v = jnp.var(x, axis=axis, keepdims=True)
    return (x - m) / jnp.sqrt(v + eps)

def _scatter_add(tgt, idx, src, axis=0):
    return tgt.at[idx].add(src)

def _segment_sum(src, seg, n):
    return jax.ops.segment_sum(src, seg, n)
kernel_name = 'mk_gnn_preln_d2_gnn_r32_ad3a25'

def setup_inputs(seed: int=0):
    np.random.seed(seed)
    _w = jnp.asarray

    def _rec_inputs():
        import jax
        import jax.numpy as jnp
        _gk = jax.random.key(seed)
        x = -0.0003713 + 1 * jax.random.normal(jax.random.fold_in(_gk, 1), (50000, 128), jnp.float32)
        src = jax.random.randint(jax.random.fold_in(_gk, 2), (50000,), 0, 50000, jnp.int32)
        dst = jax.random.randint(jax.random.fold_in(_gk, 3), (50000,), 0, 50000, jnp.int32)
        _o = jnp.argsort(dst, stable=True)
        src = src[_o]
        dst = dst[_o]
        edge_type_8 = jax.random.randint(jax.random.fold_in(_gk, 12), (50000,), 0, 8, jnp.int32)
        node_type_4 = jax.random.randint(jax.random.fold_in(_gk, 13), (50000,), 0, 4, jnp.int32)
        return (x, src, dst, edge_type_8, node_type_4)
    x, src, dst, edge_type_8, node_type_4 = _rec_inputs()

    def _L0_gnn_setup():
        import jax, jax.numpy as jnp
        import numpy as np
        N_NODES = 3125
        N_EDGES = 50000
        IN_DIM = 128
        HEADS = 4
        OUT_DIM = 32
        NEG_SLOPE = 0.2
        key = jax.random.key(seed)
        k_x, k_e, k_w, k_as, k_ad = jax.random.split(key, 5)
        x = jax.random.normal(k_x, (N_NODES, IN_DIM), dtype=jnp.float32)
        edge_index = jax.random.randint(k_e, (2, N_EDGES), 0, N_NODES, dtype=jnp.int64)
        W = jax.random.normal(k_w, (IN_DIM, HEADS * OUT_DIM), dtype=jnp.float32) / np.sqrt(IN_DIM)
        att_src = jax.random.normal(k_as, (HEADS, OUT_DIM), dtype=jnp.float32) / np.sqrt(OUT_DIM)
        att_dst = jax.random.normal(k_ad, (HEADS, OUT_DIM), dtype=jnp.float32) / np.sqrt(OUT_DIM)
        bias = jnp.zeros((HEADS * OUT_DIM,), dtype=jnp.float32)
        return {'x': x, 'edge_index': edge_index, 'W': W, 'att_src': att_src, 'att_dst': att_dst, 'bias': bias}
    _L0_gnn_all = _L0_gnn_setup()
    _L0_gnn_in = {k: v for k, v in _L0_gnn_all.items() if k in ('W', 'att_src', 'att_dst', 'bias')}
    del _L0_gnn_all

    def _L1_gnn_setup():
        import jax, jax.numpy as jnp
        import numpy as np
        import math
        HIDDEN = 128
        N_NODES = 50000
        N_EDGES = 25000
        N_NTYPES = 4
        N_ETYPES = 8

        def _type_matmul(h, W, types):
            out = jnp.zeros_like(h)
            for t in range(W.shape[0]):
                out = out + jnp.where((types == t)[:, None], h @ W[t], 0.0)
            return out

        def _sparse_softmax(scores, indices, n_segments):
            seg_max = jnp.maximum(jax.ops.segment_max(scores, indices, num_segments=n_segments), -1000000000.0)
            exp_s = jnp.exp(scores - seg_max[indices])
            seg_sum = jax.ops.segment_sum(exp_s, indices, num_segments=n_segments)
            return exp_s / (seg_sum[indices] + 1e-10)
        key = jax.random.key(seed)
        ks = jax.random.split(key, 10)
        x = jax.random.normal(ks[0], (N_NODES, HIDDEN), dtype=jnp.float32)
        edge_index = jax.random.randint(ks[1], (2, N_EDGES), 0, N_NODES, dtype=jnp.int64 if jax.config.read('jax_enable_x64') else jnp.int32)
        edge_type = jax.random.randint(ks[2], (N_EDGES,), 0, N_ETYPES, dtype=jnp.int32)
        node_type = jax.random.randint(ks[3], (N_NODES,), 0, N_NTYPES, dtype=jnp.int32)
        W_Q = jax.random.normal(ks[4], (N_NTYPES, HIDDEN, HIDDEN), dtype=jnp.float32) * 0.02
        W_K = jax.random.normal(ks[5], (N_NTYPES, HIDDEN, HIDDEN), dtype=jnp.float32) * 0.02
        W_V = jax.random.normal(ks[6], (N_NTYPES, HIDDEN, HIDDEN), dtype=jnp.float32) * 0.02
        W_edge = jax.random.normal(ks[7], (N_ETYPES, HIDDEN, HIDDEN), dtype=jnp.float32) * 0.02
        mu = jnp.ones((N_ETYPES,), dtype=jnp.float32)
        return {'x': x, 'edge_index': edge_index, 'edge_type': edge_type, 'node_type': node_type, 'W_Q': W_Q, 'W_K': W_K, 'W_V': W_V, 'W_edge': W_edge, 'mu': mu}
    _L1_gnn_all = _L1_gnn_setup()
    _L1_gnn_in = {k: v for k, v in _L1_gnn_all.items() if k in ('W_Q', 'W_K', 'W_V', 'W_edge', 'mu')}
    del _L1_gnn_all
    return {'x': x, 'src': src, 'dst': dst, 'edge_type_8': edge_type_8, 'node_type_4': node_type_4, 'L0_gnn_W': _L0_gnn_in['W'], 'L0_gnn_att_src': _L0_gnn_in['att_src'], 'L0_gnn_att_dst': _L0_gnn_in['att_dst'], 'L0_gnn_bias': _L0_gnn_in['bias'], 'L1_gnn_W_Q': _L1_gnn_in['W_Q'], 'L1_gnn_W_K': _L1_gnn_in['W_K'], 'L1_gnn_W_V': _L1_gnn_in['W_V'], 'L1_gnn_W_edge': _L1_gnn_in['W_edge'], 'L1_gnn_mu': _L1_gnn_in['mu']}

def reference(x, src, dst, edge_type_8, node_type_4, L0_gnn_W, L0_gnn_att_src, L0_gnn_att_dst, L0_gnn_bias, L1_gnn_W_Q, L1_gnn_W_K, L1_gnn_W_V, L1_gnn_W_edge, L1_gnn_mu):
    import jax
    import jax.numpy as jnp

    def _L0_gnn_ref(x, edge_index, W, att_src, att_dst, bias):
        import jax, jax.numpy as jnp
        import numpy as np
        N_NODES = 3125
        N_EDGES = 50000
        IN_DIM = 128
        HEADS = 4
        OUT_DIM = 32
        NEG_SLOPE = 0.2
        N = x.shape[0]
        H, D = att_src.shape
        loop = jnp.arange(N, dtype=edge_index.dtype)
        src = jnp.concatenate([edge_index[0], loop])
        dst = jnp.concatenate([edge_index[1], loop])
        h = (x @ W).reshape(N, H, D)
        a_src = jnp.einsum('nhd,hd->nh', h, att_src)
        a_dst = jnp.einsum('nhd,hd->nh', h, att_dst)
        e = jax.nn.leaky_relu(a_src[src] + a_dst[dst], NEG_SLOPE)
        e_max = jax.ops.segment_max(e, dst, num_segments=N)
        e_max = jnp.where(jnp.isfinite(e_max), e_max, jnp.float32(0))
        ex = jnp.exp(e - e_max[dst])
        denom = jax.ops.segment_sum(ex, dst, num_segments=N)
        alpha = ex / (denom[dst] + jnp.float32(1e-16))
        msg = h[src] * alpha[:, :, None]
        out = jax.ops.segment_sum(msg, dst, num_segments=N)
        out = out.reshape(N, H * D) + bias
        return jax.nn.elu(out)

    def _L1_gnn_ref(x, edge_index, edge_type, node_type, W_Q, W_K, W_V, W_edge, mu):
        import jax, jax.numpy as jnp
        import numpy as np
        import math
        HIDDEN = 128
        N_NODES = 50000
        N_EDGES = 25000
        N_NTYPES = 4
        N_ETYPES = 8

        def _type_matmul(h, W, types):
            out = jnp.zeros_like(h)
            for t in range(W.shape[0]):
                out = out + jnp.where((types == t)[:, None], h @ W[t], 0.0)
            return out

        def _sparse_softmax(scores, indices, n_segments):
            seg_max = jnp.maximum(jax.ops.segment_max(scores, indices, num_segments=n_segments), -1000000000.0)
            exp_s = jnp.exp(scores - seg_max[indices])
            seg_sum = jax.ops.segment_sum(exp_s, indices, num_segments=n_segments)
            return exp_s / (seg_sum[indices] + 1e-10)
        N, d = x.shape
        scale = math.sqrt(d)
        src, dst = (edge_index[0], edge_index[1])
        Q = _type_matmul(x, W_Q, node_type)
        K = _type_matmul(x, W_K, node_type)
        V = _type_matmul(x, W_V, node_type)
        q_dst = Q[dst]
        k_src = K[src]
        k_t = _type_matmul(k_src, W_edge, edge_type)
        scores = jnp.sum(q_dst * k_t, axis=-1) / scale
        scores = scores * mu[edge_type]
        attn = _sparse_softmax(scores, dst, N)
        weighted_v = V[src] * attn[:, None]
        out = jax.ops.segment_sum(weighted_v, dst, num_segments=N)
        return out
    edge_index = jnp.stack([src, dst])
    h = jnp.maximum(_layernorm(x, axis=-1), 0.0)
    x = x + _L0_gnn_ref(h, edge_index, L0_gnn_W, L0_gnn_att_src, L0_gnn_att_dst, L0_gnn_bias)
    h = jnp.maximum(_layernorm(x, axis=-1), 0.0)
    x = x + _L1_gnn_ref(h, edge_index, edge_type_8, node_type_4, L1_gnn_W_Q, L1_gnn_W_K, L1_gnn_W_V, L1_gnn_W_edge, L1_gnn_mu)
    return x

_drawn_inputs = setup_inputs


def setup_inputs(seed=0):
    import zlib

    import numpy as np

    out = dict(_drawn_inputs(seed))
    spreads = {'L0_gnn_bias': (0.0, 0.1), 'L1_gnn_mu': (1.0, 0.6)}
    factors = {'L0_gnn_att_dst': 3.186, 'L1_gnn_W_Q': 8.0, 'L1_gnn_W_K': 8.0, 'L1_gnn_W_edge': 8.0}
    for name, (base, spread) in spreads.items():
        noise = np.random.default_rng([zlib.crc32(name.encode()), seed]).standard_normal(out[name].shape)
        drawn = base * np.exp(spread * noise) if base else spread * noise
        out[name] = jnp.asarray(drawn.astype(out[name].dtype))
    for name, factor in factors.items():
        out[name] = (out[name] * factor).astype(out[name].dtype)
    return out
```

```python
from contextlib import ExitStack

import concourse.bass as bass
from concourse import mybir

P = 128
N = 50000
G = 4
NT = 392
NP = NT * P
NB = NT // G
NJ = NB // 2
ROWS = G * P
K = 4
Q = NT // K
HEADS = 4
NTYPES = 4
ETYPES = 8
BIG = 1.0e30
SKIP = float(1 << 20)

F32 = mybir.dt.float32
I32 = mybir.dt.int32
U32 = mybir.dt.uint32
ALU = mybir.AluOpType
ACT = mybir.ActivationFunctionType
AX = mybir.AxisListType


def after(eng, sem, count):
    if isinstance(count, int) and count == 0:
        return
    eng.wait_ge(sem, count)


def after_apart(eng, sem, count, turns):
    if isinstance(count, int) and count == 0:
        return
    eng.wait_ge(sem, count)
    eng.sem_inc(turns, 1)


def pairs(eng, body):
    for s in range(2):
        body(0, s)
    with eng.Fori(1, NJ) as j:
        for s in range(2):
            body(j, s)


def rows_of(table, row0, count, g=G):
    return table[bass.ds(row0, count), :].rearrange("(p g) f -> p (g f)", g=g)


def layer_norm_stats(dve, x, stats, mv, s, j, waits, stat_done, mv_done, turns):
    for g in range(G):
        dve.bn_stats(stats[s][:, g, :], x[s][:, g, :]).then_inc(stat_done[s], 1)
    after_apart(dve, stat_done[s], G * (j + 1), turns)
    for g in range(G):
        dve.bn_aggr(mv[s][:, g, :], stats[s][:, g, :]).then_inc(mv_done[s], 1)


def layer_norm_scale(pool, mv, rstd, nmr, eps, power, s, j, mv_done, sc_chain, nmr_done, turns):
    after_apart(pool, mv_done[s], G * (j + 1), turns)
    pool.tensor_tensor(rstd[s][:, 0, :], mv[s][:, :, 1], eps[:, :], ALU.add).then_inc(sc_chain[s], 1)
    after_apart(pool, sc_chain[s], 3 * j + 1, turns)
    pool.tensor_tensor(rstd[s][:, 1, :], rstd[s][:, 0, :], power[:, :], ALU.pow).then_inc(sc_chain[s], 1)
    after_apart(pool, sc_chain[s], 3 * j + 2, turns)
    pool.tensor_tensor(nmr[s][:, 0, :], mv[s][:, :, 0], rstd[s][:, 1, :], ALU.mult).then_inc(sc_chain[s], 1)
    after_apart(pool, sc_chain[s], 3 * j + 3, turns)
    pool.tensor_scalar(nmr[s][:, 1, :], nmr[s][:, 0, :], -1.0, None, ALU.mult).then_inc(nmr_done[s], 1)


def prepare(nc, sem, ident, d, keep):
    WX, WE, eps, power, sidx = keep["WX"], keep["WE"], keep["eps"], keep["power"], keep["sidx"]
    with ExitStack() as ctx:
        def sb(name, shape, dt=F32):
            return ctx.enter_context(nc.sbuf_tensor(name, shape, dt))

        ones = sb("ones", [P, P])
        att = sb("att", [P, 2, P])
        prod = sb("prod", [P, 2, P])
        mus = sb("mus", [P, ETYPES])
        wload = sb("wload", [P, ETYPES, P])
        dcol = sb("dcol", [P, NT], I32)
        dprev = sb("dprev", [P, NT], I32)
        same = sb("same", [P, NT])
        drow = sb("drow", [Q, K, P + 2], I32)
        brow = sb("brow", [Q, K, P])
        w_ld, ones_set, id_set, prod_done = sem("w_ld"), sem("ones_set"), sem("id_set"), sem("prod_done")
        mus_done, same_done, brow_done, brow_st = sem("mus_done"), sem("same_done"), sem("brow_done"), sem("brow_st")
        prep_done = sem("prep_done")
        with nc.Block() as block:
            @block.sync
            def _(sp):
                sp.dma_start(WX[:, 0:P], d["W"][:, :]).then_inc(w_ld, 16)
                sp.dma_start(att[:, 0, :], d["att_src"].broadcast_to([P, P])).then_inc(w_ld, 16)
                sp.dma_start(att[:, 1, :], d["att_dst"].broadcast_to([P, P])).then_inc(w_ld, 16)
                sp.dma_start(mus[:, :], d["mu"].broadcast_to([P, ETYPES])).then_inc(w_ld, 16)
                sp.dma_start(wload[:, :, :], d["W_edge"].rearrange("t i o -> i t o")).then_inc(w_ld, 16)
                for i, name in enumerate(("W_Q", "W_K", "W_V")):
                    sp.dma_start(keep["WN"][:, :, i * P:(i + 1) * P],
                                 d[name].rearrange("t i o -> i t o")).then_inc(w_ld, 16)
                sp.dma_start(keep["bias"][:, :], d["bias"].broadcast_to([P, P])).then_inc(w_ld, 16)
                sp.dma_start(dcol[:, :], d["dst_cols"][0, :, :]).then_inc(w_ld, 16)
                sp.dma_start(dprev[:, :], d["dst_cols"][1, :, :]).then_inc(w_ld, 16)
                sp.dma_start(drow[:, :, :], d["dst_rows"].rearrange("(k q) e -> q k e", k=K)).then_inc(w_ld, 16)
                sp.wait_ge(brow_done, 1)
                sp.dma_start(d["brow"].rearrange("(k q) e -> q k e", k=K), brow[:, :, :]).then_inc(brow_st, 16)
                sp.wait_ge(brow_st, 16)
                sp.wait_ge(w_ld, 16 * 12)

            @block.gpsimd
            def _(pool):
                pool.memset(ones[:, :], 1.0).then_inc(ones_set, 1)
                pool.wait_ge(ones_set, 1)
                pool.affine_select(out=ident[:, :], in_=ones[:, :], compare_op=ALU.is_equal, fill=0.0,
                                   base=0, pattern=[[-1, P]], channel_multiplier=1).then_inc(id_set, 1)
                pool.memset(eps[:, :], 1e-5).then_inc(id_set, 1)
                pool.memset(power[:, :], -0.5).then_inc(id_set, 1)
                pool.wait_ge(id_set, 3)

            @block.vector
            def _(dve):
                dve.wait_ge(w_ld, 16 * 12)
                for i in range(2):
                    dve.tensor_tensor(prod[:, i, :], WX[:, 0:P], att[:, i, :], ALU.mult).then_inc(prod_done, 1)
                dve.wait_ge(prod_done, 2)
                dve.tensor_reduce(WX[:, P:P + 2 * HEADS], prod[:, :, :].rearrange("p i (h e) -> p (i h) e", h=HEADS),
                                  AX.X, ALU.add).then_inc(prep_done, 1)
                dve.tensor_scalar(mus[:, :], mus[:, :], float(P) ** -0.5, None, ALU.mult).then_inc(mus_done, 1)
                dve.wait_ge(mus_done, 1)
                for t in range(ETYPES):
                    dve.tensor_scalar(WE[:, t, :], wload[:, t, :], mus[:, t:t + 1], None, ALU.mult).then_inc(prep_done, 1)
                dve.tensor_tensor(same[:, :], dcol[:, :], dprev[:, :], ALU.is_equal).then_inc(same_done, 1)
                dve.wait_ge(same_done, 1)
                dve.scalar_tensor_tensor(out=sidx[:, :], in0=same[:, :], scalar=SKIP, in1=dcol[:, :],
                                         op0=ALU.mult, op1=ALU.add).then_inc(prep_done, 1)
                dve.tensor_tensor(brow[:, :, :], drow[:, :, 1:P + 1],
                                  drow[:, :, P + 1:P + 2].broadcast_to([Q, K, P]), ALU.is_equal).then_inc(brow_done, 1)
                dve.wait_ge(prep_done, ETYPES + 2)


def project_nodes(nc, sem2, sem, ident, d, keep):
    WX = keep["WX"]
    HA = P + HEADS
    with ExitStack() as ctx:
        def sb(name, shape, dt=F32):
            return [ctx.enter_context(nc.sbuf_tensor(f"{name}{s}", shape, dt)) for s in range(2)]

        x, h, hT, rows = sb("n0_x", [P, G, P]), sb("n0_h", [P, G, P]), sb("n0_hT", [P, ROWS]), sb("n0_rows", [P, G, HA + HEADS])
        stats, mv = sb("n0_stats", [P, G, 6]), sb("n0_mv", [P, G, 2])
        rstd, nmr = sb("n0_rstd", [P, 2, G]), sb("n0_nmr", [P, 2, G])
        ad, es, drows = sb("n0_ad", [P, G, HEADS]), sb("n0_es", [P, G, HEADS]), sb("n0_drows", [P, G, 2 * HEADS])
        psT = [ctx.enter_context(nc.psum_tensor(f"n0_psT{s}", [P, ROWS], F32)) for s in range(2)]
        psH = [ctx.enter_context(nc.psum_tensor(f"n0_psH{s}", [P, G, 256], F32)) for s in range(2)]
        x_ld, stat_done, mv_done, nmr_done = sem2("n0_x_ld"), sem2("n0_stat"), sem2("n0_mv"), sem2("n0_nmr")
        sc_chain = sem2("n0_sc_chain")
        h_done, t_done, hT_done, mm_done = sem2("n0_h"), sem2("n0_t"), sem2("n0_hT"), sem2("n0_mm")
        rows_done, ad_done, es_done, drows_done = sem2("n0_rows"), sem2("n0_ad"), sem2("n0_es"), sem2("n0_drows")
        rows_st = sem2("n0_rows_st")
        turns = sem("n0_turns")
        with nc.Block() as block:
            @block.sync
            def _(sp):
                def load(j, s):
                    after(sp, h_done[s], G * j)
                    sp.dma_start(x[s][:, :, :].rearrange("p g f -> p (g f)"),
                                 rows_of(d["x"], (2 * j + s) * ROWS, ROWS)).then_inc(x_ld[s], 16)
                pairs(sp, load)

            @block.vector
            def _(dve):
                def body(j, s):
                    after_apart(dve, x_ld[s], 16 * (j + 1), turns)
                    after_apart(dve, nmr_done[s], j, turns)
                    layer_norm_stats(dve, x, stats, mv, s, j, None, stat_done, mv_done, turns)
                    dve.wait_ge(t_done[s], j + 1)
                    after(dve, mm_done[s], j)
                    dve.tensor_copy(hT[s][:, :], psT[s][:, :]).then_inc(hT_done[s], 1)
                    dve.wait_ge(rows_done[s], j + 1)
                    after(dve, rows_st[s], 32 * j)
                    dve.tensor_copy(drows[s][:, :, 0:HEADS], rows[s][:, :, HA:HA + HEADS]).then_inc(ad_done[s], 1)
                    dve.tensor_tensor(ad[s][:, :, :], rows[s][:, :, P:HA], rows[s][:, :, HA:HA + HEADS],
                                      ALU.add).then_inc(ad_done[s], 1)
                    dve.wait_ge(ad_done[s], 2 * j + 2)
                    dve.scalar_tensor_tensor(out=drows[s][:, :, HEADS:2 * HEADS], in0=ad[s][:, :, :], scalar=0.2,
                                             in1=ad[s][:, :, :], op0=ALU.mult, op1=ALU.max).then_inc(drows_done[s], 1)
                pairs(dve, body)

            @block.gpsimd
            def _(pool):
                def body(j, s):
                    after_apart(pool, h_done[s], G * j, turns)
                    layer_norm_scale(pool, mv, rstd, nmr, keep["eps"], keep["power"], s, j, mv_done, sc_chain,
                                     nmr_done, turns)
                pairs(pool, body)

            @block.scalar
            def _(act):
                def body(j, s):
                    act.wait_ge(nmr_done[s], j + 1)
                    after(act, t_done[s], j)
                    for g in range(G):
                        act.activation(h[s][:, g, :], x[s][:, g, :], ACT.Relu, bias=nmr[s][:, 1, g:g + 1],
                                       scale=rstd[s][:, 1, g:g + 1]).then_inc(h_done[s], 1)
                    act.wait_ge(mm_done[s], j + 1)
                    after(act, rows_st[s], 32 * j)
                    after(act, drows_done[s], j)
                    act.activation(rows[s][:, :, :], psH[s][:, :, 0:HA + HEADS], ACT.Copy).then_inc(rows_done[s], 1)
                    act.wait_ge(rows_done[s], j + 1)
                    act.dma_start(rows_of(d["HA"], (2 * j + s) * ROWS, ROWS).rearrange("p (g f) -> p g f", g=G),
                                  rows[s][:, :, 0:HA]).then_inc(rows_st[s], 16)
                    act.wait_ge(drows_done[s], j + 1)
                    act.dma_start(rows_of(d["D0"], (2 * j + s) * ROWS, ROWS),
                                  drows[s][:, :, :].rearrange("p g f -> p (g f)")).then_inc(rows_st[s], 16)
                pairs(act, body)
                for s in range(2):
                    act.wait_ge(rows_st[s], 32 * NJ)

            @block.tensor
            def _(pe):
                def body(j, s):
                    after(pe, hT_done[s], j)
                    for g in range(G):
                        pe.wait_ge(h_done[s], G * j + g + 1)
                        mm = pe.transpose(psT[s][:, g * P:(g + 1) * P], h[s][:, g, :], ident[:, :])
                    mm.then_inc(t_done[s], 1)
                    pe.wait_ge(hT_done[s], j + 1)
                    after(pe, rows_done[s], j)
                    for g in range(G):
                        mm = pe.matmul(psH[s][:, g, 0:P + 2 * HEADS], hT[s][:, g * P:(g + 1) * P], WX[:, :],
                                       start=True, stop=True)
                    mm.then_inc(mm_done[s], 1)
                pairs(pe, body)


def gather_scores_0(nc, sem2, sem, d, keep):
    SC, SE = keep["SC"], keep["SE"]
    HA = P + HEADS
    with ExitStack() as ctx:
        def sb(name, shape, dt=F32):
            return [ctx.enter_context(nc.sbuf_tensor(f"{name}{s}", shape, dt)) for s in range(2)]

        idx, srow, drow = sb("a0_idx", [P, 2 * G], U32), sb("a0_srow", [P, G, HA]), sb("a0_drow", [P, G, 2 * HEADS])
        raw = sb("a0_raw", [P, G, HEADS])
        zero = ctx.enter_context(nc.sbuf_tensor("a0_zero", [P, G * 136], F32))
        idx_ld, gathered, raw_done, sc_done = sem2("a0_idx_ld"), sem2("a0_gathered"), sem2("a0_raw"), sem2("a0_sc")
        msg_st, zeros_st = sem2("a0_msg_st"), sem2("a0_zeros_st")
        turns, zero_set = sem("a0_turns"), sem("a0_zero_set")
        with nc.Block() as block:
            @block.sync
            def _(sp):
                def body(j, s):
                    after(sp, gathered[s], 16 * 2 * G * j)
                    sp.dma_start(idx[s][:, :], rows_of(d["edge_idx"], (2 * j + s) * P, P, 1)).then_inc(idx_ld[s], 16)
                pairs(sp, body)

            @block.scalar
            def _(act):
                act.wait_ge(zero_set, 1)

                def body(j, s):
                    act.dma_start(rows_of(d["T0"], (2 * j + s) * ROWS, ROWS), zero[:, :]).then_inc(zeros_st[s], 16)
                    act.dma_start(rows_of(d["T1"], (2 * j + s) * ROWS, ROWS), zero[:, 0:G * 129]).then_inc(zeros_st[s], 16)
                    act.wait_ge(gathered[s], 16 * 2 * G * (j + 1))
                    act.dma_start(rows_of(d["M"], (2 * j + s) * ROWS, ROWS).rearrange("p (g f) -> p g f", g=G),
                                  srow[s][:, :, 0:P]).then_inc(msg_st[s], 16)
                pairs(act, body)
                for s in range(2):
                    act.wait_ge(msg_st[s], 16 * NJ)
                    act.wait_ge(zeros_st[s], 32 * NJ)

            @block.gpsimd
            def _(pool):
                def body(j, s):
                    after_apart(pool, idx_ld[s], 16 * (j + 1), turns)
                    after_apart(pool, msg_st[s], 16 * j, turns)
                    after_apart(pool, sc_done[s], 2 * j, turns)
                    for g in range(G):
                        pool.indirect_dma_start(srow[s][:, g, :], None, d["HA"][:, :], bass.IndirectOffsetOnAxis(
                            ap=idx[s][:, g:g + 1], axis=0)).then_inc(gathered[s], 16)
                        pool.indirect_dma_start(drow[s][:, g, :], None, d["D0"][:, :], bass.IndirectOffsetOnAxis(
                            ap=idx[s][:, G + g:G + g + 1], axis=0)).then_inc(gathered[s], 16)
                pairs(pool, body)

            @block.vector
            def _(dve):
                dve.memset(zero[:, :], 0.0).then_inc(zero_set, 1)

                def body(j, s):
                    tiles = bass.ds((2 * j + s) * G, G)
                    dve.wait_ge(gathered[s], 16 * 2 * G * (j + 1))
                    dve.tensor_tensor(raw[s][:, :, :], srow[s][:, :, P:HA], drow[s][:, :, 0:HEADS],
                                      ALU.add).then_inc(raw_done[s], 1)
                    dve.tensor_copy(SE[:, :, tiles].rearrange("p h g -> p g h"),
                                    drow[s][:, :, HEADS:2 * HEADS]).then_inc(sc_done[s], 1)
                    dve.wait_ge(raw_done[s], j + 1)
                    dve.scalar_tensor_tensor(out=SC[:, :, tiles].rearrange("p h g -> p g h"), in0=raw[s][:, :, :],
                                             scalar=0.2, in1=raw[s][:, :, :], op0=ALU.mult,
                                             op1=ALU.max).then_inc(sc_done[s], 1)
                pairs(dve, body)


def segment_softmax(nc, sem, ident, d, H, SC, SE, least, tag):
    with ExitStack() as ctx:
        def sb(name, shape, dt=F32):
            return ctx.enter_context(nc.sbuf_tensor(f"{tag}_{name}", shape, dt))

        drow = sb("drow", [Q, K, P + 2], I32)
        ends = sb("ends", [H, 2, NT + 1], I32)
        far = sb("far", [Q, 2, K, P])
        tile_far = sb("tile_far", [H, 2, NT])
        mx = sb("mx", [P, H, NT]) if SE is not None else SC
        row = sb("row", [Q, K, H, P])
        scan = [sb(f"scan{i}", [Q, K, H, P]) for i in range(2)]
        tile_end = sb("tile_end", [H, 2, NT])
        carry = sb("carry", [H, 2, NT + 1])
        carry_in = sb("carry_in", [Q, 2, K * H])
        ps = [ctx.enter_context(nc.psum_tensor(f"{tag}_ps{i}", [P, 512], F32)) for i in range(8)]
        names = ("ld", "flag", "far", "mx", "turned", "row", "scan", "end_t", "end", "carry", "in_t", "in", "scan2",
                 "max", "least", "back", "sub", "exp")
        S = {n: sem(f"{tag}_{n}") for n in names}
        with nc.Block() as block:
            @block.sync
            def _(sp):
                sp.dma_start(drow[:, :, :], d["dst_rows"].rearrange("(k q) e -> q k e", k=K)).then_inc(S["ld"], 16)
                for i in range(2):
                    sp.dma_start(ends[:, i, :], d["dst_ends"][i:i + 1, :].broadcast_to([H, NT + 1])).then_inc(S["ld"], 16)
                sp.wait_ge(S["ld"], 48)

            @block.vector
            def _(dve):
                if SE is not None:
                    dve.tensor_tensor(mx[:, :, :], SC[:, :, :], SE[:, :, :], ALU.max).then_inc(S["mx"], 1)
                dve.wait_ge(S["ld"], 48)
                for i in range(2):
                    dve.tensor_tensor(far[:, i, :, :], drow[:, :, 1:P + 1], drow[:, :, 2 * i:2 * i + P],
                                      ALU.not_equal).then_inc(S["flag"], 1)
                    dve.tensor_tensor(tile_far[:, i, :], ends[:, i, 1:NT + 1], ends[:, i, 0:NT],
                                      ALU.not_equal).then_inc(S["flag"], 1)
                dve.memset(carry[:, 0, 0:1], -BIG).then_inc(S["flag"], 1)
                dve.memset(carry[:, 1, NT:NT + 1], -BIG).then_inc(S["flag"], 1)
                dve.wait_ge(S["flag"], 6)
                dve.tensor_scalar(far[:, :, :, :], far[:, :, :, :], -BIG, None, ALU.mult).then_inc(S["far"], 1)
                dve.tensor_scalar(tile_far[:, :, :], tile_far[:, :, :], -BIG, None, ALU.mult).then_inc(S["far"], 1)
                dve.wait_ge(S["far"], 2)

                def scans(k, h, start):
                    a, b, o = far[:, :, k, :], row[:, k, h, :], [scan[i][:, k, h, :] for i in range(2)]
                    one = dve.tensor_tensor_scan(o[0], a[:, 0, :], b, start[0], op0=ALU.add, op1=ALU.max)
                    two = dve.tensor_tensor_scan(o[1][:, ::-1], a[:, 1, ::-1], b[:, ::-1], start[1], op0=ALU.add,
                                                 op1=ALU.max)
                    return one, two

                for k in range(K):
                    dve.wait_ge(S["row"], k + 1)
                    for h in range(H):
                        for ins in scans(k, h, (-BIG, -BIG)):
                            ins.then_inc(S["scan"], 1)
                dve.wait_ge(S["end"], 2)
                dve.tensor_tensor_scan(carry[:, 0, 1:NT + 1], tile_far[:, 0, :], tile_end[:, 0, :], -BIG, op0=ALU.add,
                                       op1=ALU.max).then_inc(S["carry"], 1)
                dve.tensor_tensor_scan(carry[:, 1, 0:NT][:, ::-1], tile_far[:, 1, ::-1], tile_end[:, 1, ::-1], -BIG,
                                       op0=ALU.add, op1=ALU.max).then_inc(S["carry"], 1)
                dve.wait_ge(S["in"], 1)
                for k in range(K):
                    for h in range(H):
                        c = k * H + h
                        for ins in scans(k, h, (carry_in[:, 0, c:c + 1], carry_in[:, 1, c:c + 1])):
                            ins.then_inc(S["scan2"], 1)
                dve.wait_ge(S["scan2"], 2 * K * H)
                dve.tensor_tensor(row[:, :, :, :], scan[0][:, :, :, :], scan[1][:, :, :, :], ALU.max).then_inc(S["max"], 1)
                if least is not None:
                    dve.wait_ge(S["max"], 1)
                    dve.tensor_scalar(row[:, :, :, :], row[:, :, :, :], least, None, ALU.max).then_inc(S["least"], 1)
                dve.wait_ge(S["back"], 1)
                for h in range(H):
                    dve.tensor_tensor(SC[:, h, :], SC[:, h, :], ps[h][:, 0:NT], ALU.subtract).then_inc(S["sub"], 1)
                    if SE is not None:
                        dve.tensor_tensor(SE[:, h, :], SE[:, h, :], ps[h][:, 0:NT], ALU.subtract).then_inc(S["sub"], 1)

            @block.tensor
            def _(pe):
                if SE is not None:
                    pe.wait_ge(S["mx"], 1)
                for k in range(K):
                    for h in range(H):
                        mm = pe.transpose(ps[k][0:Q, h * P:(h + 1) * P], mx[:, h, k * Q:(k + 1) * Q], ident[:, :])
                    mm.then_inc(S["turned"], 1)
                pe.wait_ge(S["scan"], 2 * K * H)
                for i in range(2):
                    for k in range(K):
                        mm = pe.transpose(ps[4 + i][0:H, k * Q:(k + 1) * Q], scan[i][:, k, :, (1 - i) * (P - 1)],
                                          ident[0:Q, 0:Q])
                    mm.then_inc(S["end_t"], 1)
                pe.wait_ge(S["carry"], 2)
                for i in range(2):
                    for k in range(K):
                        mm = pe.transpose(ps[6][0:Q, (i * K + k) * H:(i * K + k + 1) * H],
                                          carry[:, i, k * Q + i:(k + 1) * Q + i], ident[0:H, 0:H])
                mm.then_inc(S["in_t"], 1)
                pe.wait_ge(S["max"] if least is None else S["least"], 1)
                for h in range(H):
                    for k in range(K):
                        mm = pe.transpose(ps[h][:, k * Q:(k + 1) * Q], row[:, k, h, :], ident[0:Q, 0:Q])
                mm.then_inc(S["back"], 1)

            @block.scalar
            def _(act):
                for k in range(K):
                    act.wait_ge(S["turned"], k + 1)
                    act.activation(row[:, k, :, :].rearrange("q h e -> q (h e)"), ps[k][0:Q, 0:H * P],
                                   ACT.Copy).then_inc(S["row"], 1)
                for i in range(2):
                    act.wait_ge(S["end_t"], i + 1)
                    act.activation(tile_end[:, i, :], ps[4 + i][0:H, 0:NT], ACT.Copy).then_inc(S["end"], 1)
                act.wait_ge(S["in_t"], 1)
                act.activation(carry_in[:, :, :].rearrange("q i c -> q (i c)"), ps[6][0:Q, 0:2 * K * H],
                               ACT.Copy).then_inc(S["in"], 1)
                n = H * (2 if SE is not None else 1)
                act.wait_ge(S["sub"], n)
                act.activation(SC[:, :, :], SC[:, :, :], ACT.Exp).then_inc(S["exp"], 1)
                if SE is not None:
                    act.activation(SE[:, :, :], SE[:, :, :], ACT.Exp).then_inc(S["exp"], 1)
                act.wait_ge(S["exp"], 2 if SE is not None else 1)


def segment_sums(nc, sem2, sem, d, keep, H, EX, WS, table, tag):
    W = P + H
    WT = W + (H if WS is not None else 0)
    C = P // H
    with ExitStack() as ctx:
        def sb(name, shape, dt=F32):
            return [ctx.enter_context(nc.sbuf_tensor(f"{tag}_{name}{s}", shape, dt)) for s in range(2)]

        m, drow, adj, msg = sb("m", [P, G, P]), sb("drow", [P, G, P], I32), sb("adj", [P, G, P]), sb("msg", [P, G, W])
        brow, out, idx = sb("brow", [1, ROWS]), sb("out", [P, G, WT]), sb("idx", [P, G], U32)
        dcol = ctx.enter_context(nc.sbuf_tensor(f"{tag}_dcol", [P, NT], I32))
        ps = [[ctx.enter_context(nc.psum_tensor(f"{tag}_ps{s}{g}", [P, 512], F32)) for g in range(G)] for s in range(2)]
        ld, msg_done, adj_done, idx_done = sem2(f"{tag}_ld"), sem2(f"{tag}_msg"), sem2(f"{tag}_adj"), sem2(f"{tag}_idx")
        own_done, sum_done, out_done, scat = (sem2(f"{tag}_own"), sem2(f"{tag}_sum"), sem2(f"{tag}_out"),
                                              sem2(f"{tag}_scat"))
        dcol_ld, zero_set, turns = sem(f"{tag}_dcol_ld"), sem(f"{tag}_zero"), sem(f"{tag}_turns")
        outs = G + (1 if WS is not None else 0)
        with nc.Block() as block:
            @block.sync
            def _(sp):
                sp.dma_start(dcol[:, :], d["dst_cols"][0, :, :]).then_inc(dcol_ld, 16)

                def body(j, s):
                    b = j * -2 + (NB - 1 - s)
                    after_apart(sp, msg_done[s], 2 * j, turns)
                    after_apart(sp, adj_done[s], j, turns)
                    after(sp, sum_done[s], G * j)
                    sp.dma_start(m[s][:, :, :].rearrange("p g f -> p (g f)"), rows_of(d["M"], b * ROWS, ROWS)).then_inc(ld[s], 16)
                    sp.dma_start(drow[s][:, :, :].rearrange("p g e -> p (g e)"),
                                 d["dst_flat"][0:1, bass.ds(b * ROWS, ROWS)].broadcast_to([P, ROWS])).then_inc(ld[s], 16)
                    sp.dma_start(brow[s][:, :], d["brow_flat"][0:1, bass.ds(b * ROWS, ROWS)]).then_inc(ld[s], 16)
                pairs(sp, body)

            @block.vector
            def _(dve):
                dve.memset(out[1][0:1, 0, :], 0.0).then_inc(zero_set, 1)
                dve.wait_ge(dcol_ld, 16)

                def body(j, s):
                    tiles = bass.ds(j * (-2 * G) + (NT - G - G * s), G)
                    dve.wait_ge(ld[s], 48 * (j + 1))
                    after(dve, own_done[s], j)
                    dve.tensor_tensor(adj[s][:, :, :], drow[s][:, :, :],
                                      dcol[:, tiles].unsqueeze(2).broadcast_to([P, G, P]), ALU.is_equal).then_inc(adj_done[s], 1)
                    ex = EX[:, :, tiles].rearrange("p h g -> p g h")
                    if H > 1:
                        dve.tensor_tensor(msg[s][:, :, 0:P].rearrange("p g (h c) -> p g h c", h=H),
                                          m[s][:, :, :].rearrange("p g (h c) -> p g h c", h=H),
                                          ex.unsqueeze(3).broadcast_to([P, G, H, C]), ALU.mult).then_inc(msg_done[s], 1)
                    else:
                        dve.tensor_tensor(msg[s][:, :, 0:P], m[s][:, :, :], ex.broadcast_to([P, G, P]),
                                          ALU.mult).then_inc(msg_done[s], 1)
                    dve.tensor_copy(msg[s][:, :, P:W], ex).then_inc(msg_done[s], 1)
                    after(dve, scat[s], 16 * G * j)
                    dve.tensor_copy(idx[s][:, :], keep["sidx"][:, tiles]).then_inc(idx_done[s], 1)
                pairs(dve, body)

            @block.tensor
            def _(pe):
                pe.wait_ge(zero_set, 1)

                def body(j, s):
                    pe.wait_ge(msg_done[s], 2 * (j + 1))
                    pe.wait_ge(adj_done[s], j + 1)
                    after(pe, out_done[s], outs * j)
                    for g in reversed(range(G)):
                        mm = pe.matmul(ps[s][g][:, 0:W], adj[s][:, g, :], msg[s][:, g, :], start=True, stop=False)
                    mm.then_inc(own_done[s], 1)
                    for g in reversed(range(G)):
                        if g < G - 1:
                            pe.wait_ge(out_done[s], outs * j + (G - 1 - g))
                            behind = out[s][0:1, g + 1, 0:W]
                        else:
                            after(pe, out_done[1 - s], outs * (j + s))
                            behind = out[1 - s][0:1, 0, 0:W]
                        pe.matmul(ps[s][g][:, 0:W], brow[s][0:1, g * P:(g + 1) * P], behind, start=False,
                                  stop=True).then_inc(sum_done[s], 1)
                pairs(pe, body)

            @block.scalar
            def _(act):
                def body(j, s):
                    tiles = bass.ds(j * (-2 * G) + (NT - G - G * s), G)
                    after(act, scat[s], 16 * G * j)
                    for g in reversed(range(G)):
                        act.wait_ge(sum_done[s], G * j + G - g)
                        act.activation(out[s][:, g, 0:W], ps[s][g][:, 0:W], ACT.Copy).then_inc(out_done[s], 1)
                    if WS is not None:
                        act.activation(out[s][:, :, W:WT], WS[:, :, tiles].rearrange("p h g -> p g h"),
                                       ACT.Copy).then_inc(out_done[s], 1)
                pairs(act, body)

            @block.gpsimd
            def _(pool):
                def body(j, s):
                    after_apart(pool, out_done[s], outs * (j + 1), turns)
                    after_apart(pool, idx_done[s], j + 1, turns)
                    for g in range(G):
                        pool.indirect_dma_start(table[:, :], bass.IndirectOffsetOnAxis(ap=idx[s][:, g:g + 1], axis=0),
                                                out[s][:, g, :], None, bounds_check=NP - 1,
                                                oob_is_err=False).then_inc(scat[s], 16)
                pairs(pool, body)
                for s in range(2):
                    pool.wait_ge(scat[s], 16 * G * NJ)


def finish_0_project_1(nc, sem2, sem, ident, d, keep):
    HA = P + HEADS
    WT = P + 2 * HEADS
    C = P // HEADS
    with ExitStack() as ctx:
        def sb(name, shape, dt=F32):
            return [ctx.enter_context(nc.sbuf_tensor(f"n1_{name}{s}", shape, dt)) for s in range(2)]

        x, ha, t0, nt = sb("x", [P, G, P]), sb("ha", [P, G, HA]), sb("t0", [P, G, WT]), sb("nt", [P, ROWS], I32)
        tot, w, dn, r = (sb(n, [P, G, HEADS]) for n in ("tot", "w", "dn", "r"))
        u, e, x1, h = sb("u", [P, G, P]), sb("e", [P, G, P]), sb("x1", [P, G, P]), sb("h", [P, G, P])
        stats, mv = sb("stats", [P, G, 6]), sb("mv", [P, G, 2])
        rstd, nmr = sb("rstd", [P, 2, G]), sb("nmr", [P, 2, G])
        hTm = [ctx.enter_context(nc.sbuf_tensor(f"n1_hTm{s}", [P, NTYPES, ROWS], F32)) for s in range(2)]
        qkv = sb("qkv", [P, G, 3 * P])
        psT = [ctx.enter_context(nc.psum_tensor(f"n1_psT{s}", [P, ROWS], F32)) for s in range(2)]
        psQ = [ctx.enter_context(nc.psum_tensor(f"n1_psQ{g}", [P, 512], F32)) for g in range(G)]
        ld, small, wide, e_done, x1_done = sem2("n1_ld"), sem2("n1_small"), sem2("n1_wide"), sem2("n1_e"), sem2("n1_x1")
        x1_st = sem2("n1_x1_st")
        stat_done, mv_done, nmr_done, sc_chain = sem2("n1_stat"), sem2("n1_mv"), sem2("n1_nmr"), sem2("n1_sc_chain")
        h_done, t_done, hT_done, mm_done = sem2("n1_h"), sem2("n1_t"), sem2("n1_hT"), sem2("n1_mm")
        qkv_done, qkv_st = sem2("n1_qkv"), sem2("n1_qkv_st")
        turns = sem("n1_turns")
        WIDE = 5
        with nc.Block() as block:
            @block.sync
            def _(sp):
                def body(j, s):
                    row0 = (2 * j + s) * ROWS
                    after_apart(sp, x1_done[s], j, turns)
                    after(sp, hT_done[s], NTYPES * j)
                    sp.dma_start(x[s][:, :, :].rearrange("p g f -> p (g f)"), rows_of(d["x"], row0, ROWS)).then_inc(ld[s], 16)
                    sp.dma_start(ha[s][:, :, :].rearrange("p g f -> p (g f)"), rows_of(d["HA"], row0, ROWS)).then_inc(ld[s], 16)
                    sp.dma_start(t0[s][:, :, :].rearrange("p g f -> p (g f)"), rows_of(d["T0"], row0, ROWS)).then_inc(ld[s], 16)
                    sp.dma_start(nt[s][:, :], d["nt_flat"][0:1, bass.ds(row0, ROWS)].broadcast_to([P, ROWS])).then_inc(ld[s], 16)
                pairs(sp, body)

            @block.vector
            def _(dve):
                def heads(ap):
                    return ap.rearrange("p g (h c) -> p g h c", h=HEADS)

                def wide_of(ap):
                    return ap[:, :, :].unsqueeze(3).broadcast_to([P, G, HEADS, C])

                def front(j, s):
                    den, ws = t0[s][:, :, P:HA], t0[s][:, :, HA:WT]
                    dve.wait_ge(ld[s], 64 * (j + 1))
                    dve.tensor_tensor(tot[s][:, :, :], den, ws, ALU.add).then_inc(small[s], 1)
                    dve.wait_ge(small[s], 4 * j + 1)
                    dve.scalar_tensor_tensor(out=w[s][:, :, :], in0=tot[s][:, :, :], scalar=0.0, in1=ws,
                                             op0=ALU.is_equal, op1=ALU.add).then_inc(small[s], 1)
                    dve.wait_ge(small[s], 4 * j + 2)
                    dve.scalar_tensor_tensor(out=dn[s][:, :, :], in0=w[s][:, :, :], scalar=1e-16, in1=den,
                                             op0=ALU.add, op1=ALU.add).then_inc(small[s], 1)
                    dve.wait_ge(small[s], 4 * j + 3)
                    dve.reciprocal(r[s][:, :, :], dn[s][:, :, :]).then_inc(small[s], 1)
                    after(dve, x1_done[s], j)
                    dve.tensor_tensor(heads(u[s][:, :, :]), heads(ha[s][:, :, 0:P]), wide_of(w[s]), ALU.mult).then_inc(wide[s], 1)
                    dve.wait_ge(wide[s], WIDE * j + 1)
                    dve.tensor_tensor(u[s][:, :, :], u[s][:, :, :], t0[s][:, :, 0:P], ALU.add).then_inc(wide[s], 1)
                    dve.wait_ge(wide[s], WIDE * j + 2)
                    dve.wait_ge(small[s], 4 * j + 4)
                    dve.tensor_tensor(heads(u[s][:, :, :]), heads(u[s][:, :, :]), wide_of(r[s]), ALU.mult).then_inc(wide[s], 1)
                    dve.wait_ge(wide[s], WIDE * j + 3)
                    dve.tensor_tensor(u[s][:, :, :], u[s][:, :, :],
                                      keep["bias"][:, :].unsqueeze(1).broadcast_to([P, G, P]), ALU.add).then_inc(wide[s], 1)
                    dve.wait_ge(wide[s], WIDE * j + 4)
                    dve.wait_ge(e_done[s], 2 * j + 1)
                    dve.scalar_tensor_tensor(out=u[s][:, :, :], in0=u[s][:, :, :], scalar=0.0, in1=x[s][:, :, :],
                                             op0=ALU.max, op1=ALU.add).then_inc(wide[s], 1)
                    dve.tensor_scalar(e[s][:, :, :], e[s][:, :, :], 1.0, -1.0, ALU.min, ALU.add).then_inc(e_done[s], 1)
                    dve.wait_ge(wide[s], WIDE * j + 5)
                    dve.wait_ge(e_done[s], 2 * j + 2)
                    after(dve, x1_st[s], 16 * j)
                    after(dve, h_done[s], G * j)
                    dve.tensor_tensor(x1[s][:, :, :], u[s][:, :, :], e[s][:, :, :], ALU.add).then_inc(x1_done[s], 1)
                    dve.wait_ge(x1_done[s], j + 1)
                    layer_norm_stats(dve, x1, stats, mv, s, j, None, stat_done, mv_done, turns)

                def back(j, s):
                    dve.wait_ge(t_done[s], j + 1)
                    after(dve, mm_done[s], G * j)
                    for t in range(NTYPES):
                        dve.scalar_tensor_tensor(out=hTm[s][:, t, :], in0=nt[s][:, :], scalar=float(t), in1=psT[s][:, :],
                                                 op0=ALU.is_equal, op1=ALU.mult).then_inc(hT_done[s], 1)

                def body(j, s):
                    front(j, s)
                    back(j, s)
                pairs(dve, body)

            @block.gpsimd
            def _(pool):
                def body(j, s):
                    after_apart(pool, h_done[s], G * j, turns)
                    layer_norm_scale(pool, mv, rstd, nmr, keep["eps"], keep["power"], s, j, mv_done, sc_chain,
                                     nmr_done, turns)
                pairs(pool, body)

            @block.scalar
            def _(act):
                def front(j, s):
                    act.wait_ge(wide[s], WIDE * j + 4)
                    act.activation(e[s][:, :, :], u[s][:, :, :], ACT.Exp).then_inc(e_done[s], 1)
                    act.wait_ge(x1_done[s], j + 1)
                    act.dma_start(rows_of(d["X1"], (2 * j + s) * ROWS, ROWS),
                                  x1[s][:, :, :].rearrange("p g f -> p (g f)")).then_inc(x1_st[s], 16)
                    act.wait_ge(nmr_done[s], j + 1)
                    after(act, t_done[s], j)
                    for g in range(G):
                        act.activation(h[s][:, g, :], x1[s][:, g, :], ACT.Relu, bias=nmr[s][:, 1, g:g + 1],
                                       scale=rstd[s][:, 1, g:g + 1]).then_inc(h_done[s], 1)

                def back(j, s):
                    after(act, qkv_st[s], 32 * j)
                    for g in range(G):
                        act.wait_ge(mm_done[s], G * j + g + 1)
                        act.activation(qkv[s][:, g, :], psQ[g][:, 0:3 * P], ACT.Copy).then_inc(qkv_done[s], 1)
                    act.wait_ge(qkv_done[s], G * (j + 1))
                    row0 = (2 * j + s) * ROWS
                    act.dma_start(rows_of(d["QT"], row0, ROWS).rearrange("p (g f) -> p g f", g=G),
                                  qkv[s][:, :, 0:P]).then_inc(qkv_st[s], 16)
                    act.dma_start(rows_of(d["KV"], row0, ROWS).rearrange("p (g f) -> p g f", g=G),
                                  qkv[s][:, :, P:3 * P]).then_inc(qkv_st[s], 16)

                def body(j, s):
                    front(j, s)
                    back(j, s)
                pairs(act, body)
                for s in range(2):
                    act.wait_ge(x1_st[s], 16 * NJ)
                    act.wait_ge(qkv_st[s], 32 * NJ)

            @block.tensor
            def _(pe):
                def body(j, s):
                    after(pe, hT_done[s], NTYPES * j)
                    for g in range(G):
                        pe.wait_ge(h_done[s], G * j + g + 1)
                        mm = pe.transpose(psT[s][:, g * P:(g + 1) * P], h[s][:, g, :], ident[:, :])
                    mm.then_inc(t_done[s], 1)
                    pe.wait_ge(hT_done[s], NTYPES * (j + 1))
                    for g in range(G):
                        after(pe, qkv_done[1 - s], G * (j + s - 1) + g + 1) if not (isinstance(j, int) and j + s == 0) else None
                        for t in range(NTYPES):
                            mm = pe.matmul(psQ[g][:, 0:3 * P], hTm[s][:, t, g * P:(g + 1) * P], keep["WN"][:, t, :],
                                           start=(t == 0), stop=(t == NTYPES - 1))
                        mm.then_inc(mm_done[s], 1)
                pairs(pe, body)


def gather_scores_1(nc, sem2, sem, ident, d, keep):
    SC = keep["SC1"]
    with ExitStack() as ctx:
        def sb(name, shape, dt=F32):
            return [ctx.enter_context(nc.sbuf_tensor(f"a1_{name}{s}", shape, dt)) for s in range(2)]

        idx, kv, q, et = sb("idx", [P, 2 * G], U32), sb("kv", [P, G, 2 * P]), sb("q", [P, G, P]), sb("et", [P, ROWS], I32)
        kTm = sb("kTm", [P, ETYPES, ROWS])
        prod = sb("prod", [P, G, P])
        psT = [ctx.enter_context(nc.psum_tensor(f"a1_psT{s}", [P, ROWS], F32)) for s in range(2)]
        psK = [ctx.enter_context(nc.psum_tensor(f"a1_psK{s}", [P, G, P], F32)) for s in range(2)]
        idx_ld, et_ld, gathered, t_done, kT_done = (sem2("a1_idx_ld"), sem2("a1_et_ld"), sem2("a1_gathered"),
                                                    sem2("a1_t"), sem2("a1_kT"))
        mm_done, prod_done, sc_done, v_st = sem2("a1_mm"), sem2("a1_prod"), sem2("a1_sc"), sem2("a1_v_st")
        turns = sem("a1_turns")
        with nc.Block() as block:
            @block.sync
            def _(sp):
                def body(j, s):
                    after(sp, gathered[s], 16 * 2 * G * j)
                    sp.dma_start(idx[s][:, :], rows_of(d["edge_idx"], (2 * j + s) * P, P, 1)).then_inc(idx_ld[s], 16)
                    after(sp, kT_done[s], ETYPES * j)
                    sp.dma_start(et[s][:, :], d["et_flat"][0:1, bass.ds((2 * j + s) * ROWS, ROWS)].broadcast_to(
                        [P, ROWS])).then_inc(et_ld[s], 16)
                pairs(sp, body)

            @block.scalar
            def _(act):
                def body(j, s):
                    act.wait_ge(gathered[s], 16 * 2 * G * (j + 1))
                    act.dma_start(rows_of(d["M"], (2 * j + s) * ROWS, ROWS).rearrange("p (g f) -> p g f", g=G),
                                  kv[s][:, :, P:2 * P]).then_inc(v_st[s], 16)
                pairs(act, body)
                for s in range(2):
                    act.wait_ge(v_st[s], 16 * NJ)

            @block.gpsimd
            def _(pool):
                def body(j, s):
                    after_apart(pool, idx_ld[s], 16 * (j + 1), turns)
                    after_apart(pool, v_st[s], 16 * j, turns)
                    after_apart(pool, t_done[s], j, turns)
                    after_apart(pool, prod_done[s], j, turns)
                    for g in range(G):
                        pool.indirect_dma_start(kv[s][:, g, :], None, d["KV"][:, :], bass.IndirectOffsetOnAxis(
                            ap=idx[s][:, g:g + 1], axis=0)).then_inc(gathered[s], 16)
                        pool.indirect_dma_start(q[s][:, g, :], None, d["QT"][:, :], bass.IndirectOffsetOnAxis(
                            ap=idx[s][:, G + g:G + g + 1], axis=0)).then_inc(gathered[s], 16)
                pairs(pool, body)

            @block.tensor
            def _(pe):
                def body(j, s):
                    pe.wait_ge(gathered[s], 16 * 2 * G * (j + 1))
                    after(pe, kT_done[s], ETYPES * j)
                    for g in range(G):
                        mm = pe.transpose(psT[s][:, g * P:(g + 1) * P], kv[s][:, g, 0:P], ident[:, :])
                    mm.then_inc(t_done[s], 1)
                    pe.wait_ge(kT_done[s], ETYPES * (j + 1))
                    after(pe, prod_done[s], j)
                    for g in range(G):
                        for t in range(ETYPES):
                            mm = pe.matmul(psK[s][:, g, :], kTm[s][:, t, g * P:(g + 1) * P], keep["WE"][:, t, :],
                                           start=(t == 0), stop=(t == ETYPES - 1))
                    mm.then_inc(mm_done[s], 1)
                pairs(pe, body)

            @block.vector
            def _(dve):
                def body(j, s):
                    dve.wait_ge(t_done[s], j + 1)
                    dve.wait_ge(et_ld[s], 16 * (j + 1))
                    after(dve, mm_done[s], j)
                    for t in range(ETYPES):
                        dve.scalar_tensor_tensor(out=kTm[s][:, t, :], in0=et[s][:, :], scalar=float(t), in1=psT[s][:, :],
                                                 op0=ALU.is_equal, op1=ALU.mult).then_inc(kT_done[s], 1)
                    dve.wait_ge(mm_done[s], j + 1)
                    after(dve, sc_done[s], j)
                    dve.tensor_tensor(prod[s][:, :, :], q[s][:, :, :], psK[s][:, :, :], ALU.mult).then_inc(prod_done[s], 1)
                    dve.wait_ge(prod_done[s], j + 1)
                    dve.tensor_reduce(SC[:, 0, bass.ds((2 * j + s) * G, G)], prod[s][:, :, :], AX.X,
                                      ALU.add).then_inc(sc_done[s], 1)
                pairs(dve, body)


def finish_1(nc, sem2, sem, d):
    with ExitStack() as ctx:
        def sb(name, shape, dt=F32):
            return [ctx.enter_context(nc.sbuf_tensor(f"n2_{name}{s}", shape, dt)) for s in range(2)]

        x1, t1, dn, r, u, o = (sb("x1", [P, G, P]), sb("t1", [P, G, P + 1]), sb("dn", [P, G, 1]), sb("r", [P, G, 1]),
                               sb("u", [P, G, P]), sb("o", [P, G, P]))
        ld, dn_done, r_done, u_done, o_done, o_st = (sem2("n2_ld"), sem2("n2_dn"), sem2("n2_r"), sem2("n2_u"),
                                                     sem2("n2_o"), sem2("n2_o_st"))
        with nc.Block() as block:
            @block.sync
            def _(sp):
                def body(j, s):
                    row0 = (2 * j + s) * ROWS
                    after(sp, o_done[s], j)
                    sp.dma_start(x1[s][:, :, :].rearrange("p g f -> p (g f)"), rows_of(d["X1"], row0, ROWS)).then_inc(ld[s], 16)
                    sp.dma_start(t1[s][:, :, :].rearrange("p g f -> p (g f)"), rows_of(d["T1"], row0, ROWS)).then_inc(ld[s], 16)
                pairs(sp, body)

            @block.vector
            def _(dve):
                def body(j, s):
                    dve.wait_ge(ld[s], 32 * (j + 1))
                    dve.tensor_scalar(dn[s][:, :, :], t1[s][:, :, P:P + 1], 1e-10, None, ALU.add).then_inc(dn_done[s], 1)
                    dve.wait_ge(dn_done[s], j + 1)
                    dve.reciprocal(r[s][:, :, :], dn[s][:, :, :]).then_inc(r_done[s], 1)
                    dve.wait_ge(r_done[s], j + 1)
                    dve.tensor_tensor(u[s][:, :, :], t1[s][:, :, 0:P], r[s][:, :, :].broadcast_to([P, G, P]),
                                      ALU.mult).then_inc(u_done[s], 1)
                    dve.wait_ge(u_done[s], j + 1)
                    after(dve, o_st[s], 16 * j)
                    dve.tensor_tensor(o[s][:, :, :], u[s][:, :, :], x1[s][:, :, :], ALU.add).then_inc(o_done[s], 1)
                pairs(dve, body)

            @block.scalar
            def _(act):
                def body(j, s):
                    act.wait_ge(o_done[s], j + 1)
                    act.dma_start(rows_of(d["out"], (2 * j + s) * ROWS, ROWS),
                                  o[s][:, :, :].rearrange("p g f -> p (g f)")).then_inc(o_st[s], 16)
                pairs(act, body)
                for s in range(2):
                    act.wait_ge(o_st[s], 16 * NJ)


def gnn(nc, d):
    for name, shape in (("HA", (NP, P + HEADS)), ("D0", (NP, 2 * HEADS)), ("M", (NP, P)), ("T0", (NP, P + 2 * HEADS)),
                        ("T1", (NP, P + 1)), ("X1", (NP, P)), ("QT", (NP, P)), ("KV", (NP, 2 * P)), ("brow", (NT, P))):
        d[name] = nc.dram_tensor(f"scratch_{name}", shape, F32, kind="Internal").ap()
    d["brow_flat"] = d["brow"].rearrange("(o t) e -> o (t e)", o=1)
    with ExitStack() as ctx:
        def sb(name, shape, dt=F32):
            return ctx.enter_context(nc.sbuf_tensor(name, shape, dt))

        held = []

        def sem(name):
            held.append(nc.alloc_semaphore(name=name))
            return held[-1]

        def sem2(name):
            return [sem(f"{name}_slot{s}") for s in range(2)]

        def phase_ends():
            nc.clear_and_free_semaphores(held)
            nc.all_engine_barrier()
            held.clear()

        ident = sb("ident", [P, P])
        keep = {
            "WX": sb("WX", [P, P + 2 * HEADS]), "WE": sb("WE", [P, ETYPES, P]), "WN": sb("WN", [P, NTYPES, 3 * P]),
            "bias": sb("bias", [P, P]), "eps": sb("eps", [P, G]), "power": sb("power", [P, G]),
            "sidx": sb("sidx", [P, NT], U32), "SC": sb("SC", [P, HEADS, NT]), "SE": sb("SE", [P, HEADS, NT]),
            "SC1": sb("SC1", [P, 1, NT]),
        }
        prepare(nc, sem, ident, d, keep)
        phase_ends()
        project_nodes(nc, sem2, sem, ident, d, keep)
        phase_ends()
        gather_scores_0(nc, sem2, sem, d, keep)
        phase_ends()
        segment_softmax(nc, sem, ident, d, HEADS, keep["SC"], keep["SE"], None, "s0")
        phase_ends()
        segment_sums(nc, sem2, sem, d, keep, HEADS, keep["SC"], keep["SE"], d["T0"], "b0")
        phase_ends()
        finish_0_project_1(nc, sem2, sem, ident, d, keep)
        phase_ends()
        gather_scores_1(nc, sem2, sem, ident, d, keep)
        phase_ends()
        segment_softmax(nc, sem, ident, d, 1, keep["SC1"], None, -1.0e9, "s1")
        phase_ends()
        segment_sums(nc, sem2, sem, d, keep, 1, keep["SC1"], None, d["T1"], "b1")
        phase_ends()
        finish_1(nc, sem2, sem, d)
        phase_ends()


def kernel(x, src, dst, edge_type_8, node_type_4, L0_gnn_W, L0_gnn_att_src, L0_gnn_att_dst, L0_gnn_bias,
           L1_gnn_W_Q, L1_gnn_W_K, L1_gnn_W_V, L1_gnn_W_edge, L1_gnn_mu):
    import numpy as np
    import concourse.bacc as bacc
    from concourse.bass_utils import run_bass_kernel_spmd

    def padded(a, fill):
        a = np.asarray(a)
        return np.concatenate([a, np.full((NP - N,) + a.shape[1:], fill, a.dtype)])

    src_p, dst_p = padded(src, 0), padded(dst, N)
    before = np.concatenate([np.full(1, N + 2, dst_p.dtype), dst_p[:-1]])
    behind = np.concatenate([dst_p[1:], np.full(1, N + 1, dst_p.dtype)])
    tiles, tiles_before, tiles_behind = (a.reshape(NT, P) for a in (dst_p, before, behind))
    arrays = {
        "x": padded(x, 0.0),
        "edge_idx": np.concatenate([a.reshape(NB, G, P).transpose(0, 2, 1) for a in (src_p, dst_p)],
                                   axis=2).reshape(NB * P, 2 * G).astype(src_p.dtype),
        "dst_cols": np.stack([tiles.T, tiles_before.T]),
        "dst_rows": np.concatenate([tiles_before[:, :1], tiles, tiles_behind[:, -1:]], axis=1),
        "dst_ends": np.stack([np.concatenate([before[:1], tiles[:, -1]]), np.concatenate([tiles[:, 0], behind[-1:]])]),
        "dst_flat": dst_p.reshape(1, NP),
        "et_flat": padded(edge_type_8, 0).reshape(1, NP),
        "nt_flat": padded(node_type_4, 0).reshape(NB, P, G).transpose(0, 2, 1).reshape(1, NP),
        "W": L0_gnn_W, "att_src": np.asarray(L0_gnn_att_src).reshape(1, P),
        "att_dst": np.asarray(L0_gnn_att_dst).reshape(1, P), "bias": np.asarray(L0_gnn_bias).reshape(1, P),
        "W_Q": L1_gnn_W_Q, "W_K": L1_gnn_W_K, "W_V": L1_gnn_W_V, "W_edge": L1_gnn_W_edge,
        "mu": np.asarray(L1_gnn_mu).reshape(1, ETYPES),
    }
    nc = bacc.Bacc("TRN2", target_bir_lowering=False, num_devices=1)
    given, d = {}, {}
    for name, a in arrays.items():
        a = np.ascontiguousarray(a)
        given[f"in_{name}"] = a
        dt = U32 if name == "edge_idx" else mybir.dt.from_np(a.dtype)
        d[name] = nc.dram_tensor(f"in_{name}", a.shape, dt, kind="ExternalInput").ap()
    d["out"] = nc.dram_tensor("out_0", (NP, P), F32, kind="ExternalOutput").ap()
    gnn(nc, d)
    r = run_bass_kernel_spmd(nc, [given], core_ids=[0])
    return r.results[0]["out_0"][:N]
```

```python
from contextlib import ExitStack

import concourse.bass as bass
from concourse import mybir

P = 128
N = 50000
G = 4
NT = 392
NP = NT * P
NB = NT // G
U = 4
ROWS = G * P
K = 4
Q = NT // K
HEADS = 4
NTYPES = 4
ETYPES = 8
BIG = 1.0e30
SKIP = float(1 << 20)

F32 = mybir.dt.float32
I32 = mybir.dt.int32
U32 = mybir.dt.uint32
ALU = mybir.AluOpType
ACT = mybir.ActivationFunctionType
AX = mybir.AxisListType


class Batch:

    def __init__(self, m, c):
        self.m, self.c = m, c

    def slot(self, n):
        return self.c % n

    def turn(self, n):
        return self.m * (U // n) + self.c // n

    def before(self, n):
        return Batch(self.m, self.c - n)

    def at(self, size, offset=0):
        return self.m * (U * size) + (self.c * size + offset)


def staged(eng, *stages):
    last_lag = max(lag for lag, _ in stages)
    first = -(-(U + last_lag) // U) * U
    turns = NB // U

    def step(n):
        for lag, work in stages:
            if 0 <= n - lag < NB:
                work(Batch((n - lag) // U, (n - lag) % U))

    for n in range(first):
        step(n)
    with eng.Fori(first // U, turns) as m:
        for r in range(U):
            for lag, work in stages:
                back = (r - lag) // U
                work(Batch(m + back if back else m, (r - lag) % U))
    for n in range(turns * U, NB + last_lag):
        step(n)


def wait(eng, sems, batch, per=1, part=None, apart=None):
    if isinstance(batch.m, int) and U * batch.m + batch.c < 0:
        return
    n = len(sems)
    eng.wait_ge(sems[batch.slot(n)], batch.turn(n) * per + (per if part is None else part))
    if apart is not None:
        eng.sem_inc(apart, 1)


def all_landed(eng, sems, per):
    n = len(sems)
    for s in range(n):
        eng.wait_ge(sems[s], per * len(range(s, NB, n)))


def rows_of(table, row0, count=ROWS, g=G):
    return table[bass.ds(row0, count), :].rearrange("(p g) f -> p (g f)", g=g)


def parts_of(table, row0):
    return rows_of(table, row0).rearrange("p (g f) -> p g f", g=G)


def flat(tile):
    return tile[:, :, :].rearrange("p g f -> p (g f)")


def layer_norm_stats(dve, b, x, stats, mv, stat_done, mv_done, turns):
    for g in range(G):
        dve.bn_stats(stats[:, g, :], x[:, g, :]).then_inc(stat_done[0], 1)
    wait(dve, stat_done, b, G, apart=turns)
    for g in range(G):
        dve.bn_aggr(mv[:, g, :], stats[:, g, :]).then_inc(mv_done[0], 1)


def layer_norm_scale(pool, b, mv, rstd, nmr, keep, mv_done, chain, nmr_done, turns):
    wait(pool, mv_done, b, G, apart=turns)
    pool.tensor_tensor(rstd[:, 0, :], mv[:, :, 1], keep["eps"][:, :], ALU.add).then_inc(chain[0], 1)
    pool.tensor_scalar(nmr[:, 0, :], mv[:, :, 0], -1.0, None, ALU.mult).then_inc(chain[0], 1)
    wait(pool, chain, b, 3, 2, apart=turns)
    pool.tensor_tensor(rstd[:, 1, :], rstd[:, 0, :], keep["power"][:, :], ALU.pow).then_inc(chain[0], 1)
    wait(pool, chain, b, 3, 3, apart=turns)
    pool.tensor_tensor(nmr[:, 1, :], nmr[:, 0, :], rstd[:, 1, :], ALU.mult).then_inc(nmr_done[0], 1)


def prepare(nc, sem, ident, d, keep):
    WX, WE, eps, power, sidx = keep["WX"], keep["WE"], keep["eps"], keep["power"], keep["sidx"]
    with ExitStack() as ctx:
        def sb(name, shape, dt=F32):
            return ctx.enter_context(nc.sbuf_tensor(name, shape, dt))

        ones = sb("ones", [P, P])
        att = sb("att", [P, 2, P])
        prod = sb("prod", [P, 2, P])
        mus = sb("mus", [P, ETYPES])
        wload = sb("wload", [P, ETYPES, P])
        dcol = sb("dcol", [P, NT], I32)
        dprev = sb("dprev", [P, NT], I32)
        same = sb("same", [P, NT])
        drow = sb("drow", [Q, K, P + 2], I32)
        brow = sb("brow", [Q, K, P])
        w_ld, ones_set, id_set, prod_done = sem("w_ld"), sem("ones_set"), sem("id_set"), sem("prod_done")
        mus_done, same_done, brow_done, brow_st = sem("mus_done"), sem("same_done"), sem("brow_done"), sem("brow_st")
        prep_done = sem("prep_done")
        with nc.Block() as block:
            @block.sync
            def _(sp):
                sp.dma_start(WX[:, 0:P], d["W"][:, :]).then_inc(w_ld, 16)
                sp.dma_start(att[:, 0, :], d["att_src"].broadcast_to([P, P])).then_inc(w_ld, 16)
                sp.dma_start(att[:, 1, :], d["att_dst"].broadcast_to([P, P])).then_inc(w_ld, 16)
                sp.dma_start(mus[:, :], d["mu"].broadcast_to([P, ETYPES])).then_inc(w_ld, 16)
                sp.dma_start(wload[:, :, :], d["W_edge"].rearrange("t i o -> i t o")).then_inc(w_ld, 16)
                for i, name in enumerate(("W_Q", "W_K", "W_V")):
                    sp.dma_start(keep["WN"][:, :, i * P:(i + 1) * P],
                                 d[name].rearrange("t i o -> i t o")).then_inc(w_ld, 16)
                sp.dma_start(keep["bias"][:, :], d["bias"].broadcast_to([P, P])).then_inc(w_ld, 16)
                sp.dma_start(dcol[:, :], d["dst_cols"][0, :, :]).then_inc(w_ld, 16)
                sp.dma_start(dprev[:, :], d["dst_cols"][1, :, :]).then_inc(w_ld, 16)
                sp.dma_start(drow[:, :, :], d["dst_rows"].rearrange("(k q) e -> q k e", k=K)).then_inc(w_ld, 16)
                sp.wait_ge(brow_done, 1)
                sp.dma_start(d["brow"].rearrange("(k q) e -> q k e", k=K), brow[:, :, :]).then_inc(brow_st, 16)
                sp.wait_ge(brow_st, 16)
                sp.wait_ge(w_ld, 16 * 12)

            @block.gpsimd
            def _(pool):
                pool.memset(ones[:, :], 1.0).then_inc(ones_set, 1)
                pool.wait_ge(ones_set, 1)
                pool.affine_select(out=ident[:, :], in_=ones[:, :], compare_op=ALU.is_equal, fill=0.0,
                                   base=0, pattern=[[-1, P]], channel_multiplier=1).then_inc(id_set, 1)
                pool.memset(eps[:, :], 1e-5).then_inc(id_set, 1)
                pool.memset(power[:, :], -0.5).then_inc(id_set, 1)
                pool.wait_ge(id_set, 3)

            @block.vector
            def _(dve):
                dve.wait_ge(w_ld, 16 * 12)
                for i in range(2):
                    dve.tensor_tensor(prod[:, i, :], WX[:, 0:P], att[:, i, :], ALU.mult).then_inc(prod_done, 1)
                dve.wait_ge(prod_done, 2)
                dve.tensor_reduce(WX[:, P:P + 2 * HEADS], prod[:, :, :].rearrange("p i (h e) -> p (i h) e", h=HEADS),
                                  AX.X, ALU.add).then_inc(prep_done, 1)
                dve.tensor_scalar(mus[:, :], mus[:, :], float(P) ** -0.5, None, ALU.mult).then_inc(mus_done, 1)
                dve.wait_ge(mus_done, 1)
                for t in range(ETYPES):
                    dve.tensor_scalar(WE[:, t, :], wload[:, t, :], mus[:, t:t + 1], None, ALU.mult).then_inc(prep_done, 1)
                dve.tensor_tensor(same[:, :], dcol[:, :], dprev[:, :], ALU.is_equal).then_inc(same_done, 1)
                dve.wait_ge(same_done, 1)
                dve.scalar_tensor_tensor(out=sidx[:, :], in0=same[:, :], scalar=SKIP, in1=dcol[:, :],
                                         op0=ALU.mult, op1=ALU.add).then_inc(prep_done, 1)
                dve.tensor_tensor(brow[:, :, :], drow[:, :, 1:P + 1],
                                  drow[:, :, P + 1:P + 2].broadcast_to([Q, K, P]), ALU.is_equal).then_inc(brow_done, 1)
                dve.wait_ge(prep_done, ETYPES + 2)


def project_nodes(nc, one, ring, ident, d, keep):
    WX = keep["WX"]
    HA = P + HEADS
    with ExitStack() as ctx:
        def sb(n, name, shape, dt=F32):
            return [ctx.enter_context(nc.sbuf_tensor(f"n0_{name}{s}", shape, dt)) for s in range(n)]

        x, h, hT, rows = sb(4, "x", [P, G, P]), sb(2, "h", [P, G, P]), sb(2, "hT", [P, ROWS]), sb(4, "rows", [P, G, HA + HEADS])
        stats, mv = sb(4, "stats", [P, G, 6]), sb(4, "mv", [P, G, 2])
        rstd, nmr = sb(4, "rstd", [P, 2, G]), sb(4, "nmr", [P, 2, G])
        ad, drows = sb(4, "ad", [P, G, HEADS]), sb(4, "drows", [P, G, 2 * HEADS])
        psT = [ctx.enter_context(nc.psum_tensor(f"n0_psT{s}", [P, ROWS], F32)) for s in range(2)]
        psH = [ctx.enter_context(nc.psum_tensor(f"n0_psH{s}", [P, G, 256], F32)) for s in range(2)]
        x_ld, rows_st, drows_st = ring("n0_x_ld", 4), ring("n0_rows_st", 4), ring("n0_drows_st", 4)
        stat_done, mv_done, chain, nmr_done = one("n0_stat"), one("n0_mv"), one("n0_chain"), one("n0_nmr")
        h_done, t_done, hT_done, mm_done = one("n0_h"), one("n0_t"), one("n0_hT"), one("n0_mm")
        rows_done, ad_done, drows_done, turns = one("n0_rows"), one("n0_ad"), one("n0_drows"), one("n0_turns")[0]
        with nc.Block() as block:
            @block.sync
            def _(sp):
                def load(b):
                    wait(sp, h_done, b.before(4), G)
                    sp.dma_start(flat(x[b.slot(4)]), rows_of(d["x"], b.at(ROWS))).then_inc(x_ld[b.slot(4)], 16)

                def store(b):
                    wait(sp, rows_done, b)
                    sp.dma_start(parts_of(d["HA"], b.at(ROWS)), rows[b.slot(4)][:, :, 0:HA]).then_inc(rows_st[b.slot(4)], 16)

                def store_scores(b):
                    wait(sp, drows_done, b)
                    sp.dma_start(rows_of(d["D0"], b.at(ROWS)), flat(drows[b.slot(4)])).then_inc(drows_st[b.slot(4)], 16)
                staged(sp, (0, load), (3, store), (5, store_scores))
                all_landed(sp, rows_st, 16)
                all_landed(sp, drows_st, 16)

            @block.vector
            def _(dve):
                def moments(b):
                    wait(dve, x_ld, b, 16, apart=turns)
                    wait(dve, nmr_done, b.before(4), apart=turns)
                    layer_norm_stats(dve, b, x[b.slot(4)], stats[b.slot(4)], mv[b.slot(4)], stat_done, mv_done, turns)

                def turned(b):
                    wait(dve, t_done, b)
                    wait(dve, mm_done, b.before(2))
                    dve.tensor_copy(hT[b.slot(2)][:, :], psT[b.slot(2)][:, :]).then_inc(hT_done[0], 1)

                def self_scores(b):
                    r, a, dr = rows[b.slot(4)], ad[b.slot(4)], drows[b.slot(4)]
                    wait(dve, rows_done, b)
                    wait(dve, drows_st, b.before(4), 16)
                    dve.tensor_copy(dr[:, :, 0:HEADS], r[:, :, HA:HA + HEADS]).then_inc(ad_done[0], 1)
                    dve.tensor_tensor(a[:, :, :], r[:, :, P:HA], r[:, :, HA:HA + HEADS], ALU.add).then_inc(ad_done[0], 1)
                    wait(dve, ad_done, b, 2)
                    dve.scalar_tensor_tensor(out=dr[:, :, HEADS:2 * HEADS], in0=a[:, :, :], scalar=0.2,
                                             in1=a[:, :, :], op0=ALU.mult, op1=ALU.max).then_inc(drows_done[0], 1)
                staged(dve, (0, moments), (2, turned), (4, self_scores))

            @block.gpsimd
            def _(pool):
                def scale(b):
                    wait(pool, h_done, b.before(4), G, apart=turns)
                    layer_norm_scale(pool, b, mv[b.slot(4)], rstd[b.slot(4)], nmr[b.slot(4)], keep, mv_done, chain,
                                     nmr_done, turns)
                staged(pool, (0, scale))

            @block.scalar
            def _(act):
                def normalise(b):
                    wait(act, nmr_done, b)
                    wait(act, t_done, b.before(2))
                    for g in range(G):
                        act.activation(h[b.slot(2)][:, g, :], x[b.slot(4)][:, g, :], ACT.Relu,
                                       bias=nmr[b.slot(4)][:, 1, g:g + 1],
                                       scale=rstd[b.slot(4)][:, 1, g:g + 1]).then_inc(h_done[0], 1)

                def products(b):
                    wait(act, mm_done, b)
                    wait(act, rows_st, b.before(4), 16)
                    wait(act, drows_done, b.before(4))
                    act.activation(rows[b.slot(4)][:, :, :], psH[b.slot(2)][:, :, 0:HA + HEADS],
                                   ACT.Copy).then_inc(rows_done[0], 1)
                staged(act, (0, normalise), (2, products))

            @block.tensor
            def _(pe):
                def turn(b):
                    wait(pe, hT_done, b.before(2))
                    for g in range(G):
                        wait(pe, h_done, b, G, g + 1)
                        mm = pe.transpose(psT[b.slot(2)][:, g * P:(g + 1) * P], h[b.slot(2)][:, g, :], ident[:, :])
                    mm.then_inc(t_done[0], 1)

                def project(b):
                    wait(pe, hT_done, b)
                    wait(pe, rows_done, b.before(2))
                    for g in range(G):
                        mm = pe.matmul(psH[b.slot(2)][:, g, 0:P + 2 * HEADS], hT[b.slot(2)][:, g * P:(g + 1) * P],
                                       WX[:, :], start=True, stop=True)
                    mm.then_inc(mm_done[0], 1)
                staged(pe, (0, turn), (1, project))


def gather_scores_0(nc, one, ring, d, keep):
    SC, SE = keep["SC"], keep["SE"]
    HA = P + HEADS
    with ExitStack() as ctx:
        def sb(n, name, shape, dt=F32):
            return [ctx.enter_context(nc.sbuf_tensor(f"a0_{name}{s}", shape, dt)) for s in range(n)]

        idx, srow, drow = sb(4, "idx", [P, 2 * G], U32), sb(4, "srow", [P, G, HA]), sb(4, "drow", [P, G, 2 * HEADS])
        raw = sb(2, "raw", [P, G, HEADS])
        zero = sb(1, "zero", [P, G * (P + 2 * HEADS)])[0]
        idx_ld, gathered, msg_st, zeros_st = (ring("a0_idx_ld", 4), ring("a0_gathered", 4), ring("a0_msg_st", 4),
                                              ring("a0_zeros_st", 4))
        raw_done, sc_done, zero_set, turns = one("a0_raw"), one("a0_sc"), one("a0_zero_set")[0], one("a0_turns")[0]
        with nc.Block() as block:
            @block.sync
            def _(sp):
                def load(b):
                    wait(sp, gathered, b.before(4), 16 * 2 * G)
                    sp.dma_start(idx[b.slot(4)][:, :], rows_of(d["edge_idx"], b.at(P), P, 1)).then_inc(idx_ld[b.slot(4)], 16)
                staged(sp, (0, load))

            @block.scalar
            def _(act):
                act.wait_ge(zero_set, 1)

                def store(b):
                    act.dma_start(rows_of(d["T0"], b.at(ROWS)), zero[:, :]).then_inc(zeros_st[b.slot(4)], 16)
                    act.dma_start(rows_of(d["T1"], b.at(ROWS)), zero[:, 0:G * (P + 1)]).then_inc(zeros_st[b.slot(4)], 16)
                    wait(act, gathered, b, 16 * 2 * G)
                    act.dma_start(parts_of(d["M"], b.at(ROWS)), srow[b.slot(4)][:, :, 0:P]).then_inc(msg_st[b.slot(4)], 16)
                staged(act, (0, store))
                all_landed(act, msg_st, 16)
                all_landed(act, zeros_st, 32)

            @block.gpsimd
            def _(pool):
                def gather(b):
                    i = idx[b.slot(4)]
                    wait(pool, idx_ld, b, 16, apart=turns)
                    wait(pool, msg_st, b.before(4), 16, apart=turns)
                    wait(pool, sc_done, b.before(4), 2, apart=turns)
                    for g in range(G):
                        pool.indirect_dma_start(srow[b.slot(4)][:, g, :], None, d["HA"][:, :], bass.IndirectOffsetOnAxis(
                            ap=i[:, g:g + 1], axis=0)).then_inc(gathered[b.slot(4)], 16)
                        pool.indirect_dma_start(drow[b.slot(4)][:, g, :], None, d["D0"][:, :], bass.IndirectOffsetOnAxis(
                            ap=i[:, G + g:G + g + 1], axis=0)).then_inc(gathered[b.slot(4)], 16)
                staged(pool, (0, gather))

            @block.vector
            def _(dve):
                dve.memset(zero[:, :], 0.0).then_inc(zero_set, 1)

                def score(b):
                    sr, dr, r = srow[b.slot(4)], drow[b.slot(4)], raw[b.slot(2)]
                    tiles = bass.ds(b.at(G), G)
                    wait(dve, gathered, b, 16 * 2 * G)
                    dve.tensor_tensor(r[:, :, :], sr[:, :, P:HA], dr[:, :, 0:HEADS], ALU.add).then_inc(raw_done[0], 1)
                    dve.tensor_copy(SE[:, :, tiles].rearrange("p h g -> p g h"),
                                    dr[:, :, HEADS:2 * HEADS]).then_inc(sc_done[0], 1)
                    wait(dve, raw_done, b)
                    dve.scalar_tensor_tensor(out=SC[:, :, tiles].rearrange("p h g -> p g h"), in0=r[:, :, :],
                                             scalar=0.2, in1=r[:, :, :], op0=ALU.mult,
                                             op1=ALU.max).then_inc(sc_done[0], 1)
                staged(dve, (0, score))


def segment_softmax(nc, sem, ident, d, H, SC, SE, least, tag):
    with ExitStack() as ctx:
        def sb(name, shape, dt=F32):
            return ctx.enter_context(nc.sbuf_tensor(f"{tag}_{name}", shape, dt))

        drow = sb("drow", [Q, K, P + 2], I32)
        ends = sb("ends", [H, 2, NT + 1], I32)
        far = sb("far", [Q, 2, K, P])
        tile_far = sb("tile_far", [H, 2, NT])
        mx = sb("mx", [P, H, NT]) if SE is not None else SC
        row = sb("row", [Q, K, H, P])
        scan = [sb(f"scan{i}", [Q, K, H, P]) for i in range(2)]
        tile_end = sb("tile_end", [H, 2, NT])
        carry = sb("carry", [H, 2, NT + 1])
        carry_in = sb("carry_in", [Q, 2, K * H])
        ps = [ctx.enter_context(nc.psum_tensor(f"{tag}_ps{i}", [P, 512], F32)) for i in range(8)]
        names = ("ld", "flag", "far", "mx", "turned", "row", "scan", "end_t", "end", "carry", "in_t", "in", "scan2",
                 "max", "least", "back", "sub", "exp")
        S = {n: sem(f"{tag}_{n}") for n in names}
        with nc.Block() as block:
            @block.sync
            def _(sp):
                sp.dma_start(drow[:, :, :], d["dst_rows"].rearrange("(k q) e -> q k e", k=K)).then_inc(S["ld"], 16)
                for i in range(2):
                    sp.dma_start(ends[:, i, :], d["dst_ends"][i:i + 1, :].broadcast_to([H, NT + 1])).then_inc(S["ld"], 16)
                sp.wait_ge(S["ld"], 48)

            @block.vector
            def _(dve):
                if SE is not None:
                    dve.tensor_tensor(mx[:, :, :], SC[:, :, :], SE[:, :, :], ALU.max).then_inc(S["mx"], 1)
                dve.wait_ge(S["ld"], 48)
                for i in range(2):
                    dve.tensor_tensor(far[:, i, :, :], drow[:, :, 1:P + 1], drow[:, :, 2 * i:2 * i + P],
                                      ALU.not_equal).then_inc(S["flag"], 1)
                    dve.tensor_tensor(tile_far[:, i, :], ends[:, i, 1:NT + 1], ends[:, i, 0:NT],
                                      ALU.not_equal).then_inc(S["flag"], 1)
                dve.memset(carry[:, 0, 0:1], -BIG).then_inc(S["flag"], 1)
                dve.memset(carry[:, 1, NT:NT + 1], -BIG).then_inc(S["flag"], 1)
                dve.wait_ge(S["flag"], 6)
                dve.tensor_scalar(far[:, :, :, :], far[:, :, :, :], -BIG, None, ALU.mult).then_inc(S["far"], 1)
                dve.tensor_scalar(tile_far[:, :, :], tile_far[:, :, :], -BIG, None, ALU.mult).then_inc(S["far"], 1)
                dve.wait_ge(S["far"], 2)

                def scans(k, h, start):
                    a, b, o = far[:, :, k, :], row[:, k, h, :], [scan[i][:, k, h, :] for i in range(2)]
                    one = dve.tensor_tensor_scan(o[0], a[:, 0, :], b, start[0], op0=ALU.add, op1=ALU.max)
                    two = dve.tensor_tensor_scan(o[1][:, ::-1], a[:, 1, ::-1], b[:, ::-1], start[1], op0=ALU.add,
                                                 op1=ALU.max)
                    return one, two

                for k in range(K):
                    dve.wait_ge(S["row"], k + 1)
                    for h in range(H):
                        for ins in scans(k, h, (-BIG, -BIG)):
                            ins.then_inc(S["scan"], 1)
                dve.wait_ge(S["end"], 2)
                dve.tensor_tensor_scan(carry[:, 0, 1:NT + 1], tile_far[:, 0, :], tile_end[:, 0, :], -BIG, op0=ALU.add,
                                       op1=ALU.max).then_inc(S["carry"], 1)
                dve.tensor_tensor_scan(carry[:, 1, 0:NT][:, ::-1], tile_far[:, 1, ::-1], tile_end[:, 1, ::-1], -BIG,
                                       op0=ALU.add, op1=ALU.max).then_inc(S["carry"], 1)
                dve.wait_ge(S["in"], 1)
                for k in range(K):
                    for h in range(H):
                        c = k * H + h
                        for ins in scans(k, h, (carry_in[:, 0, c:c + 1], carry_in[:, 1, c:c + 1])):
                            ins.then_inc(S["scan2"], 1)
                dve.wait_ge(S["scan2"], 2 * K * H)
                dve.tensor_tensor(row[:, :, :, :], scan[0][:, :, :, :], scan[1][:, :, :, :], ALU.max).then_inc(S["max"], 1)
                if least is not None:
                    dve.wait_ge(S["max"], 1)
                    dve.tensor_scalar(row[:, :, :, :], row[:, :, :, :], least, None, ALU.max).then_inc(S["least"], 1)
                dve.wait_ge(S["back"], 1)
                for h in range(H):
                    dve.tensor_tensor(SC[:, h, :], SC[:, h, :], ps[h][:, 0:NT], ALU.subtract).then_inc(S["sub"], 1)
                    if SE is not None:
                        dve.tensor_tensor(SE[:, h, :], SE[:, h, :], ps[h][:, 0:NT], ALU.subtract).then_inc(S["sub"], 1)

            @block.tensor
            def _(pe):
                if SE is not None:
                    pe.wait_ge(S["mx"], 1)
                for k in range(K):
                    for h in range(H):
                        mm = pe.transpose(ps[k][0:Q, h * P:(h + 1) * P], mx[:, h, k * Q:(k + 1) * Q], ident[:, :])
                    mm.then_inc(S["turned"], 1)
                pe.wait_ge(S["scan"], 2 * K * H)
                for i in range(2):
                    for k in range(K):
                        mm = pe.transpose(ps[4 + i][0:H, k * Q:(k + 1) * Q], scan[i][:, k, :, (1 - i) * (P - 1)],
                                          ident[0:Q, 0:Q])
                    mm.then_inc(S["end_t"], 1)
                pe.wait_ge(S["carry"], 2)
                for i in range(2):
                    for k in range(K):
                        mm = pe.transpose(ps[6][0:Q, (i * K + k) * H:(i * K + k + 1) * H],
                                          carry[:, i, k * Q + i:(k + 1) * Q + i], ident[0:H, 0:H])
                mm.then_inc(S["in_t"], 1)
                pe.wait_ge(S["max"] if least is None else S["least"], 1)
                for h in range(H):
                    for k in range(K):
                        mm = pe.transpose(ps[h][:, k * Q:(k + 1) * Q], row[:, k, h, :], ident[0:Q, 0:Q])
                mm.then_inc(S["back"], 1)

            @block.scalar
            def _(act):
                for k in range(K):
                    act.wait_ge(S["turned"], k + 1)
                    act.activation(row[:, k, :, :].rearrange("q h e -> q (h e)"), ps[k][0:Q, 0:H * P],
                                   ACT.Copy).then_inc(S["row"], 1)
                for i in range(2):
                    act.wait_ge(S["end_t"], i + 1)
                    act.activation(tile_end[:, i, :], ps[4 + i][0:H, 0:NT], ACT.Copy).then_inc(S["end"], 1)
                act.wait_ge(S["in_t"], 1)
                act.activation(carry_in[:, :, :].rearrange("q i c -> q (i c)"), ps[6][0:Q, 0:2 * K * H],
                               ACT.Copy).then_inc(S["in"], 1)
                n = H * (2 if SE is not None else 1)
                act.wait_ge(S["sub"], n)
                act.activation(SC[:, :, :], SC[:, :, :], ACT.Exp).then_inc(S["exp"], 1)
                if SE is not None:
                    act.activation(SE[:, :, :], SE[:, :, :], ACT.Exp).then_inc(S["exp"], 1)
                act.wait_ge(S["exp"], 2 if SE is not None else 1)


def segment_sums(nc, one, ring, d, keep, H, EX, WS, table, tag):
    W = P + H
    WT = W + (H if WS is not None else 0)
    C = P // H
    outs = G + (1 if WS is not None else 0)
    with ExitStack() as ctx:
        def sb(n, name, shape, dt=F32):
            return [ctx.enter_context(nc.sbuf_tensor(f"{tag}_{name}{s}", shape, dt)) for s in range(n)]

        m, drow, brow = sb(4, "m", [P, G, P]), sb(4, "drow", [P, G, P], I32), sb(4, "brow", [1, ROWS])
        adj, msg, carry = sb(2, "adj", [P, G, P]), sb(2, "msg", [P, G, W]), sb(4, "carry", [1, G, W])
        out, idx, dcol = sb(4, "out", [P, G, WT]), sb(4, "idx", [P, G], U32), sb(1, "dcol", [P, NT], I32)[0]
        ps = [[ctx.enter_context(nc.psum_tensor(f"{tag}_ps{s}{g}", [P, 512], F32)) for g in range(G)] for s in range(2)]
        ld, scat = ring(f"{tag}_ld", 4), ring(f"{tag}_scat", 4)
        msg_done, adj_done, idx_done, own_done = one(f"{tag}_msg"), one(f"{tag}_adj"), one(f"{tag}_idx"), one(f"{tag}_own")
        sum_done, carry_done, out_done = one(f"{tag}_sum"), one(f"{tag}_carry"), one(f"{tag}_out")
        dcol_ld, zero_set, turns = one(f"{tag}_dcol_ld")[0], one(f"{tag}_zero")[0], one(f"{tag}_turns")[0]
        LAST = NT - G
        with nc.Block() as block:
            @block.sync
            def _(sp):
                sp.dma_start(dcol[:, :], d["dst_cols"][0, :, :]).then_inc(dcol_ld, 16)

                def load(b):
                    s, row0 = b.slot(4), b.at(-ROWS, LAST * P)
                    wait(sp, msg_done, b.before(4), 2, apart=turns)
                    wait(sp, adj_done, b.before(4), apart=turns)
                    wait(sp, sum_done, b.before(4), G, apart=turns)
                    sp.dma_start(flat(m[s]), rows_of(d["M"], row0)).then_inc(ld[s], 16)
                    sp.dma_start(flat(drow[s]), d["dst_flat"][0:1, bass.ds(row0, ROWS)].broadcast_to([P, ROWS])).then_inc(ld[s], 16)
                    sp.dma_start(brow[s][:, :], d["brow_flat"][0:1, bass.ds(row0, ROWS)]).then_inc(ld[s], 16)
                staged(sp, (0, load))

            @block.vector
            def _(dve):
                dve.memset(carry[3][:, 0, :], 0.0).then_inc(zero_set, 1)
                dve.wait_ge(dcol_ld, 16)

                def weigh(b):
                    tiles = bass.ds(b.at(-G, LAST), G)
                    loaded, ad, ms = m[b.slot(4)], adj[b.slot(2)], msg[b.slot(2)]
                    wait(dve, ld, b, 48)
                    wait(dve, own_done, b.before(2))
                    dve.tensor_tensor(ad[:, :, :], drow[b.slot(4)][:, :, :],
                                      dcol[:, tiles].unsqueeze(2).broadcast_to([P, G, P]), ALU.is_equal).then_inc(adj_done[0], 1)
                    ex = EX[:, :, tiles].rearrange("p h g -> p g h")
                    if H > 1:
                        dve.tensor_tensor(ms[:, :, 0:P].rearrange("p g (h c) -> p g h c", h=H),
                                          loaded[:, :, :].rearrange("p g (h c) -> p g h c", h=H),
                                          ex.unsqueeze(3).broadcast_to([P, G, H, C]), ALU.mult).then_inc(msg_done[0], 1)
                    else:
                        dve.tensor_tensor(ms[:, :, 0:P], loaded[:, :, :], ex.broadcast_to([P, G, P]),
                                          ALU.mult).then_inc(msg_done[0], 1)
                    dve.tensor_copy(ms[:, :, P:W], ex).then_inc(msg_done[0], 1)
                    wait(dve, scat, b.before(4), 16 * G)
                    dve.tensor_copy(idx[b.slot(4)][:, :], keep["sidx"][:, tiles]).then_inc(idx_done[0], 1)

                def hand_on(b):
                    wait(dve, own_done, b, apart=turns)
                    wait(dve, ld, b, 48, apart=turns)
                    wait(dve, sum_done, b.before(3), G, apart=turns)
                    for g in reversed(range(G)):
                        incoming = carry[b.slot(4)][:, g + 1, :] if g < G - 1 else carry[b.before(1).slot(4)][:, 0, :]
                        if g < G - 1:
                            wait(dve, carry_done, b, G, G - 1 - g)
                        else:
                            wait(dve, carry_done, b.before(1), G)
                        dve.scalar_tensor_tensor(out=carry[b.slot(4)][:, g, :], in0=incoming,
                                                 scalar=brow[b.slot(4)][:, g * P:g * P + 1],
                                                 in1=ps[b.slot(2)][g][0:1, 0:W], op0=ALU.mult,
                                                 op1=ALU.add).then_inc(carry_done[0], 1)
                staged(dve, (0, weigh), (1, hand_on))

            @block.tensor
            def _(pe):
                pe.wait_ge(zero_set, 1)

                def own(b):
                    wait(pe, msg_done, b, 2)
                    wait(pe, adj_done, b)
                    wait(pe, out_done, b.before(2), outs)
                    for g in reversed(range(G)):
                        mm = pe.matmul(ps[b.slot(2)][g][:, 0:W], adj[b.slot(2)][:, g, :], msg[b.slot(2)][:, g, :],
                                       start=True, stop=True)
                    mm.then_inc(own_done[0], 1)

                def behind(b):
                    wait(pe, carry_done, b, G)
                    for g in reversed(range(G)):
                        row = carry[b.slot(4)][:, g + 1, :] if g < G - 1 else carry[b.before(1).slot(4)][:, 0, :]
                        pe.matmul(ps[b.slot(2)][g][:, 0:W], brow[b.slot(4)][:, g * P:(g + 1) * P], row, start=False,
                                  stop=True, skip_group_check=True).then_inc(sum_done[0], 1)
                staged(pe, (0, own), (1, behind))

            @block.scalar
            def _(act):
                def take(b):
                    o = out[b.slot(4)]
                    wait(act, scat, b.before(4), 16 * G)
                    if WS is not None:
                        act.activation(o[:, :, W:WT], WS[:, :, bass.ds(b.at(-G, LAST), G)].rearrange("p h g -> p g h"),
                                       ACT.Copy).then_inc(out_done[0], 1)
                    for g in reversed(range(G)):
                        wait(act, sum_done, b, G, G - g)
                        act.activation(o[:, g, 0:W], ps[b.slot(2)][g][:, 0:W], ACT.Copy).then_inc(out_done[0], 1)
                staged(act, (0, take))

            @block.gpsimd
            def _(pool):
                def scatter(b):
                    wait(pool, idx_done, b, apart=turns)
                    wait(pool, out_done, b, outs, apart=turns)
                    for g in reversed(range(G)):
                        pool.indirect_dma_start(table[:, :], bass.IndirectOffsetOnAxis(ap=idx[b.slot(4)][:, g:g + 1], axis=0),
                                                out[b.slot(4)][:, g, :], None, bounds_check=NP - 1,
                                                oob_is_err=False).then_inc(scat[b.slot(4)], 16)
                staged(pool, (0, scatter))
                all_landed(pool, scat, 16 * G)


def finish_0_project_1(nc, one, ring, ident, d, keep):
    HA = P + HEADS
    WT = P + 2 * HEADS
    C = P // HEADS
    with ExitStack() as ctx:
        def sb(n, name, shape, dt=F32):
            return [ctx.enter_context(nc.sbuf_tensor(f"n1_{name}{s}", shape, dt)) for s in range(n)]

        x, ha, t0, nt = sb(4, "x", [P, G, P]), sb(4, "ha", [P, G, HA]), sb(4, "t0", [P, G, WT]), sb(4, "nt", [P, ROWS], I32)
        tot, w, dn, r = (sb(2, n, [P, G, HEADS]) for n in ("tot", "w", "dn", "r"))
        u, e, x1, h = sb(2, "u", [P, G, P]), sb(2, "e", [P, G, P]), sb(4, "x1", [P, G, P]), sb(2, "h", [P, G, P])
        stats, mv = sb(4, "stats", [P, G, 6]), sb(4, "mv", [P, G, 2])
        rstd, nmr = sb(4, "rstd", [P, 2, G]), sb(4, "nmr", [P, 2, G])
        hTm, qkv = sb(2, "hTm", [P, NTYPES, ROWS]), sb(4, "qkv", [P, G, 3 * P])
        psT = [ctx.enter_context(nc.psum_tensor(f"n1_psT{s}", [P, ROWS], F32)) for s in range(2)]
        psQ = [ctx.enter_context(nc.psum_tensor(f"n1_psQ{g}", [P, 512], F32)) for g in range(G)]
        ld, x1_st, qkv_st = ring("n1_ld", 4), ring("n1_x1_st", 4), ring("n1_qkv_st", 4)
        small, wide, exp_done, e_done, x1_done = one("n1_small"), one("n1_wide"), one("n1_exp"), one("n1_e"), one("n1_x1")
        stat_done, mv_done, chain, nmr_done = one("n1_stat"), one("n1_mv"), one("n1_chain"), one("n1_nmr")
        h_done, t_done, hT_done, mm_done = one("n1_h"), one("n1_t"), one("n1_hT"), one("n1_mm")
        xu_done, qkv_done, turns = one("n1_xu"), one("n1_qkv"), one("n1_turns")[0]
        WIDE = 4
        with nc.Block() as block:
            @block.sync
            def _(sp):
                def load(b):
                    row0, s = b.at(ROWS), b.slot(4)
                    wait(sp, x1_done, b.before(4), apart=turns)
                    wait(sp, hT_done, b.before(4), NTYPES, apart=turns)
                    sp.dma_start(flat(x[s]), rows_of(d["x"], row0)).then_inc(ld[s], 16)
                    sp.dma_start(flat(ha[s]), rows_of(d["HA"], row0)).then_inc(ld[s], 16)
                    sp.dma_start(flat(t0[s]), rows_of(d["T0"], row0)).then_inc(ld[s], 16)
                    sp.dma_start(nt[s][:, :], d["nt_flat"][0:1, bass.ds(row0, ROWS)].broadcast_to([P, ROWS])).then_inc(ld[s], 16)

                def store_x1(b):
                    wait(sp, x1_done, b)
                    sp.dma_start(rows_of(d["X1"], b.at(ROWS)), flat(x1[b.slot(4)])).then_inc(x1_st[b.slot(4)], 16)

                def store_qkv(b):
                    wait(sp, qkv_done, b, G)
                    sp.dma_start(parts_of(d["QT"], b.at(ROWS)), qkv[b.slot(4)][:, :, 0:P]).then_inc(qkv_st[b.slot(4)], 16)
                    sp.dma_start(parts_of(d["KV"], b.at(ROWS)), qkv[b.slot(4)][:, :, P:3 * P]).then_inc(qkv_st[b.slot(4)], 16)
                staged(sp, (0, load), (2, store_x1), (4, store_qkv))
                all_landed(sp, x1_st, 16)
                all_landed(sp, qkv_st, 32)

            @block.vector
            def _(dve):
                def heads(ap):
                    return ap.rearrange("p g (h c) -> p g h c", h=HEADS)

                def spread(ap):
                    return ap[:, :, :].unsqueeze(3).broadcast_to([P, G, HEADS, C])

                def combine(b):
                    t, two = t0[b.slot(4)], b.slot(2)
                    den, ws = t[:, :, P:HA], t[:, :, HA:WT]
                    uu = u[two][:, :, :]
                    wait(dve, ld, b, 64)
                    dve.tensor_tensor(tot[two][:, :, :], den, ws, ALU.add).then_inc(small[0], 1)
                    wait(dve, small, b, 4, 1)
                    dve.scalar_tensor_tensor(out=w[two][:, :, :], in0=tot[two][:, :, :], scalar=0.0, in1=ws,
                                             op0=ALU.is_equal, op1=ALU.add).then_inc(small[0], 1)
                    wait(dve, small, b, 4, 2)
                    dve.scalar_tensor_tensor(out=dn[two][:, :, :], in0=w[two][:, :, :], scalar=1e-16, in1=den,
                                             op0=ALU.add, op1=ALU.add).then_inc(small[0], 1)
                    dve.tensor_tensor(heads(uu), heads(ha[b.slot(4)][:, :, 0:P]), spread(w[two]), ALU.mult).then_inc(wide[0], 1)
                    wait(dve, small, b, 4, 3)
                    dve.reciprocal(r[two][:, :, :], dn[two][:, :, :]).then_inc(small[0], 1)
                    wait(dve, wide, b, WIDE, 1)
                    dve.tensor_tensor(uu, uu, t[:, :, 0:P], ALU.add).then_inc(wide[0], 1)
                    wait(dve, wide, b, WIDE, 2)
                    wait(dve, small, b, 4, 4)
                    dve.tensor_tensor(heads(uu), heads(uu), spread(r[two]), ALU.mult).then_inc(wide[0], 1)
                    wait(dve, wide, b, WIDE, 3)
                    dve.tensor_tensor(uu, uu, keep["bias"][:, :].unsqueeze(1).broadcast_to([P, G, P]),
                                      ALU.add).then_inc(wide[0], 1)

                def residual(b):
                    two, four = b.slot(2), b.slot(4)
                    wait(dve, wide, b, WIDE, 4)
                    wait(dve, exp_done, b)
                    dve.tensor_scalar(e[two][:, :, :], e[two][:, :, :], 1.0, -1.0, ALU.min, ALU.add).then_inc(e_done[0], 1)
                    dve.scalar_tensor_tensor(out=u[two][:, :, :], in0=u[two][:, :, :], scalar=0.0, in1=x[four][:, :, :],
                                             op0=ALU.max, op1=ALU.add).then_inc(xu_done[0], 1)
                    wait(dve, xu_done, b)
                    wait(dve, e_done, b)
                    wait(dve, x1_st, b.before(4), 16)
                    wait(dve, h_done, b.before(4), G)
                    dve.tensor_tensor(x1[four][:, :, :], u[two][:, :, :], e[two][:, :, :], ALU.add).then_inc(x1_done[0], 1)
                    wait(dve, x1_done, b, apart=turns)
                    layer_norm_stats(dve, b, x1[four], stats[four], mv[four], stat_done, mv_done, turns)

                def by_type(b):
                    wait(dve, t_done, b)
                    wait(dve, mm_done, b.before(2), G)
                    for t in range(NTYPES):
                        dve.scalar_tensor_tensor(out=hTm[b.slot(2)][:, t, :], in0=nt[b.slot(4)][:, :], scalar=float(t),
                                                 in1=psT[b.slot(2)][:, :], op0=ALU.is_equal,
                                                 op1=ALU.mult).then_inc(hT_done[0], 1)
                staged(dve, (0, combine), (1, residual), (2, by_type))

            @block.gpsimd
            def _(pool):
                def scale(b):
                    wait(pool, h_done, b.before(4), G, apart=turns)
                    layer_norm_scale(pool, b, mv[b.slot(4)], rstd[b.slot(4)], nmr[b.slot(4)], keep, mv_done, chain,
                                     nmr_done, turns)
                staged(pool, (0, scale))

            @block.scalar
            def _(act):
                def exponential(b):
                    wait(act, wide, b, WIDE, 4)
                    wait(act, x1_done, b.before(2))
                    act.activation(e[b.slot(2)][:, :, :], u[b.slot(2)][:, :, :], ACT.Exp).then_inc(exp_done[0], 1)

                def normalise(b):
                    wait(act, nmr_done, b)
                    wait(act, t_done, b.before(2))
                    for g in range(G):
                        act.activation(h[b.slot(2)][:, g, :], x1[b.slot(4)][:, g, :], ACT.Relu,
                                       bias=nmr[b.slot(4)][:, 1, g:g + 1],
                                       scale=rstd[b.slot(4)][:, 1, g:g + 1]).then_inc(h_done[0], 1)

                def products(b):
                    wait(act, qkv_st, b.before(4), 32)
                    for g in range(G):
                        wait(act, mm_done, b, G, g + 1)
                        act.activation(qkv[b.slot(4)][:, g, :], psQ[g][:, 0:3 * P], ACT.Copy).then_inc(qkv_done[0], 1)
                staged(act, (0, exponential), (1, normalise), (3, products))

            @block.tensor
            def _(pe):
                def turn(b):
                    wait(pe, hT_done, b.before(2), NTYPES)
                    for g in range(G):
                        wait(pe, h_done, b, G, g + 1)
                        mm = pe.transpose(psT[b.slot(2)][:, g * P:(g + 1) * P], h[b.slot(2)][:, g, :], ident[:, :])
                    mm.then_inc(t_done[0], 1)

                def project(b):
                    wait(pe, hT_done, b, NTYPES)
                    for g in range(G):
                        wait(pe, qkv_done, b.before(1), G, g + 1)
                        for t in range(NTYPES):
                            mm = pe.matmul(psQ[g][:, 0:3 * P], hTm[b.slot(2)][:, t, g * P:(g + 1) * P], keep["WN"][:, t, :],
                                           start=(t == 0), stop=(t == NTYPES - 1))
                        mm.then_inc(mm_done[0], 1)
                staged(pe, (0, turn), (1, project))


def gather_scores_1(nc, one, ring, ident, d, keep):
    SC = keep["SC1"]
    with ExitStack() as ctx:
        def sb(n, name, shape, dt=F32):
            return [ctx.enter_context(nc.sbuf_tensor(f"a1_{name}{s}", shape, dt)) for s in range(n)]

        idx, kv, q, et = (sb(4, "idx", [P, 2 * G], U32), sb(4, "kv", [P, G, 2 * P]), sb(4, "q", [P, G, P]),
                          sb(4, "et", [P, ROWS], I32))
        kTm, prod = sb(2, "kTm", [P, ETYPES, ROWS]), sb(2, "prod", [P, G, P])
        psT = [ctx.enter_context(nc.psum_tensor(f"a1_psT{s}", [P, ROWS], F32)) for s in range(2)]
        psK = [ctx.enter_context(nc.psum_tensor(f"a1_psK{s}", [P, G, P], F32)) for s in range(2)]
        idx_ld, et_ld, gathered, v_st = ring("a1_idx_ld", 4), ring("a1_et_ld", 4), ring("a1_gathered", 4), ring("a1_v_st", 4)
        t_done, kT_done, mm_done, prod_done, sc_done = one("a1_t"), one("a1_kT"), one("a1_mm"), one("a1_prod"), one("a1_sc")
        turns = one("a1_turns")[0]
        with nc.Block() as block:
            @block.sync
            def _(sp):
                def load(b):
                    wait(sp, gathered, b.before(4), 16 * 2 * G)
                    sp.dma_start(idx[b.slot(4)][:, :], rows_of(d["edge_idx"], b.at(P), P, 1)).then_inc(idx_ld[b.slot(4)], 16)
                    wait(sp, kT_done, b.before(4), ETYPES)
                    sp.dma_start(et[b.slot(4)][:, :], d["et_flat"][0:1, bass.ds(b.at(ROWS), ROWS)].broadcast_to(
                        [P, ROWS])).then_inc(et_ld[b.slot(4)], 16)
                staged(sp, (0, load))

            @block.scalar
            def _(act):
                def store(b):
                    wait(act, gathered, b, 16 * 2 * G)
                    act.dma_start(parts_of(d["M"], b.at(ROWS)), kv[b.slot(4)][:, :, P:2 * P]).then_inc(v_st[b.slot(4)], 16)
                staged(act, (0, store))
                all_landed(act, v_st, 16)

            @block.gpsimd
            def _(pool):
                def gather(b):
                    i = idx[b.slot(4)]
                    wait(pool, idx_ld, b, 16, apart=turns)
                    wait(pool, v_st, b.before(4), 16, apart=turns)
                    wait(pool, t_done, b.before(4), apart=turns)
                    wait(pool, prod_done, b.before(4), apart=turns)
                    for g in range(G):
                        pool.indirect_dma_start(kv[b.slot(4)][:, g, :], None, d["KV"][:, :], bass.IndirectOffsetOnAxis(
                            ap=i[:, g:g + 1], axis=0)).then_inc(gathered[b.slot(4)], 16)
                        pool.indirect_dma_start(q[b.slot(4)][:, g, :], None, d["QT"][:, :], bass.IndirectOffsetOnAxis(
                            ap=i[:, G + g:G + g + 1], axis=0)).then_inc(gathered[b.slot(4)], 16)
                staged(pool, (0, gather))

            @block.tensor
            def _(pe):
                def turn(b):
                    wait(pe, gathered, b, 16 * 2 * G)
                    wait(pe, kT_done, b.before(2), ETYPES)
                    for g in range(G):
                        mm = pe.transpose(psT[b.slot(2)][:, g * P:(g + 1) * P], kv[b.slot(4)][:, g, 0:P], ident[:, :])
                    mm.then_inc(t_done[0], 1)

                def through_edges(b):
                    wait(pe, prod_done, b.before(2))
                    wait(pe, kT_done, b, ETYPES)
                    for g in range(G):
                        for t in range(ETYPES):
                            mm = pe.matmul(psK[b.slot(2)][:, g, :], kTm[b.slot(2)][:, t, g * P:(g + 1) * P],
                                           keep["WE"][:, t, :], start=(t == 0), stop=(t == ETYPES - 1))
                    mm.then_inc(mm_done[0], 1)
                staged(pe, (0, turn), (1, through_edges))

            @block.vector
            def _(dve):
                def by_type(b):
                    wait(dve, t_done, b)
                    wait(dve, et_ld, b, 16)
                    wait(dve, mm_done, b.before(2))
                    for t in range(ETYPES):
                        dve.scalar_tensor_tensor(out=kTm[b.slot(2)][:, t, :], in0=et[b.slot(4)][:, :], scalar=float(t),
                                                 in1=psT[b.slot(2)][:, :], op0=ALU.is_equal,
                                                 op1=ALU.mult).then_inc(kT_done[0], 1)

                def score(b):
                    wait(dve, mm_done, b)
                    wait(dve, sc_done, b.before(2))
                    dve.tensor_tensor(prod[b.slot(2)][:, :, :], q[b.slot(4)][:, :, :], psK[b.slot(2)][:, :, :],
                                      ALU.mult).then_inc(prod_done[0], 1)
                    wait(dve, prod_done, b)
                    dve.tensor_reduce(SC[:, 0, bass.ds(b.at(G), G)], prod[b.slot(2)][:, :, :], AX.X,
                                      ALU.add).then_inc(sc_done[0], 1)
                staged(dve, (0, by_type), (1, score))


def finish_1(nc, one, ring, d):
    with ExitStack() as ctx:
        def sb(n, name, shape, dt=F32):
            return [ctx.enter_context(nc.sbuf_tensor(f"n2_{name}{s}", shape, dt)) for s in range(n)]

        x1, t1, dn, r, u, o = (sb(4, "x1", [P, G, P]), sb(4, "t1", [P, G, P + 1]), sb(2, "dn", [P, G, 1]),
                               sb(2, "r", [P, G, 1]), sb(2, "u", [P, G, P]), sb(4, "o", [P, G, P]))
        ld, o_st = ring("n2_ld", 4), ring("n2_o_st", 4)
        dn_done, r_done, u_done, o_done = one("n2_dn"), one("n2_r"), one("n2_u"), one("n2_o")
        with nc.Block() as block:
            @block.sync
            def _(sp):
                def load(b):
                    wait(sp, o_done, b.before(4))
                    sp.dma_start(flat(x1[b.slot(4)]), rows_of(d["X1"], b.at(ROWS))).then_inc(ld[b.slot(4)], 16)
                    sp.dma_start(flat(t1[b.slot(4)]), rows_of(d["T1"], b.at(ROWS))).then_inc(ld[b.slot(4)], 16)
                staged(sp, (0, load))

            @block.vector
            def _(dve):
                def divide(b):
                    two, t = b.slot(2), t1[b.slot(4)]
                    wait(dve, ld, b, 32)
                    dve.tensor_scalar(dn[two][:, :, :], t[:, :, P:P + 1], 1e-10, None, ALU.add).then_inc(dn_done[0], 1)
                    wait(dve, dn_done, b)
                    dve.reciprocal(r[two][:, :, :], dn[two][:, :, :]).then_inc(r_done[0], 1)
                    wait(dve, r_done, b)
                    dve.tensor_tensor(u[two][:, :, :], t[:, :, 0:P], r[two][:, :, :].broadcast_to([P, G, P]),
                                      ALU.mult).then_inc(u_done[0], 1)
                    wait(dve, u_done, b)
                    wait(dve, o_st, b.before(4), 16)
                    dve.tensor_tensor(o[b.slot(4)][:, :, :], u[two][:, :, :], x1[b.slot(4)][:, :, :],
                                      ALU.add).then_inc(o_done[0], 1)
                staged(dve, (0, divide))

            @block.scalar
            def _(act):
                def store(b):
                    wait(act, o_done, b)
                    act.dma_start(rows_of(d["out"], b.at(ROWS)), flat(o[b.slot(4)])).then_inc(o_st[b.slot(4)], 16)
                staged(act, (0, store))
                all_landed(act, o_st, 16)


def gnn(nc, d):
    for name, shape in (("HA", (NP, P + HEADS)), ("D0", (NP, 2 * HEADS)), ("M", (NP, P)), ("T0", (NP, P + 2 * HEADS)),
                        ("T1", (NP, P + 1)), ("X1", (NP, P)), ("QT", (NP, P)), ("KV", (NP, 2 * P)), ("brow", (NT, P))):
        d[name] = nc.dram_tensor(f"scratch_{name}", shape, F32, kind="Internal").ap()
    d["brow_flat"] = d["brow"].rearrange("(o t) e -> o (t e)", o=1)
    with ExitStack() as ctx:
        def sb(name, shape, dt=F32):
            return ctx.enter_context(nc.sbuf_tensor(name, shape, dt))

        held = []

        def sem(name):
            held.append(nc.alloc_semaphore(name=name))
            return held[-1]

        def one(name):
            return [sem(name)]

        def ring(name, n):
            return [sem(f"{name}_{i}") for i in range(n)]

        def phase_ends():
            nc.clear_and_free_semaphores(held)
            nc.all_engine_barrier()
            held.clear()

        ident = sb("ident", [P, P])
        keep = {
            "WX": sb("WX", [P, P + 2 * HEADS]), "WE": sb("WE", [P, ETYPES, P]), "WN": sb("WN", [P, NTYPES, 3 * P]),
            "bias": sb("bias", [P, P]), "eps": sb("eps", [P, G]), "power": sb("power", [P, G]),
            "sidx": sb("sidx", [P, NT], U32), "SC": sb("SC", [P, HEADS, NT]), "SE": sb("SE", [P, HEADS, NT]),
            "SC1": sb("SC1", [P, 1, NT]),
        }
        prepare(nc, sem, ident, d, keep)
        phase_ends()
        project_nodes(nc, one, ring, ident, d, keep)
        phase_ends()
        gather_scores_0(nc, one, ring, d, keep)
        phase_ends()
        segment_softmax(nc, sem, ident, d, HEADS, keep["SC"], keep["SE"], None, "s0")
        phase_ends()
        segment_sums(nc, one, ring, d, keep, HEADS, keep["SC"], keep["SE"], d["T0"], "b0")
        phase_ends()
        finish_0_project_1(nc, one, ring, ident, d, keep)
        phase_ends()
        gather_scores_1(nc, one, ring, ident, d, keep)
        phase_ends()
        segment_softmax(nc, sem, ident, d, 1, keep["SC1"], None, -1.0e9, "s1")
        phase_ends()
        segment_sums(nc, one, ring, d, keep, 1, keep["SC1"], None, d["T1"], "b1")
        phase_ends()
        finish_1(nc, one, ring, d)
        phase_ends()


def kernel(x, src, dst, edge_type_8, node_type_4, L0_gnn_W, L0_gnn_att_src, L0_gnn_att_dst, L0_gnn_bias,
           L1_gnn_W_Q, L1_gnn_W_K, L1_gnn_W_V, L1_gnn_W_edge, L1_gnn_mu):
    import numpy as np
    import concourse.bacc as bacc
    from concourse.bass_utils import run_bass_kernel_spmd

    def padded(a, fill):
        a = np.asarray(a)
        return np.concatenate([a, np.full((NP - N,) + a.shape[1:], fill, a.dtype)])

    src_p, dst_p = padded(src, 0), padded(dst, N)
    before = np.concatenate([np.full(1, N + 2, dst_p.dtype), dst_p[:-1]])
    behind = np.concatenate([dst_p[1:], np.full(1, N + 1, dst_p.dtype)])
    tiles, tiles_before, tiles_behind = (a.reshape(NT, P) for a in (dst_p, before, behind))
    arrays = {
        "x": padded(x, 0.0),
        "edge_idx": np.concatenate([a.reshape(NB, G, P).transpose(0, 2, 1) for a in (src_p, dst_p)],
                                   axis=2).reshape(NB * P, 2 * G).astype(src_p.dtype),
        "dst_cols": np.stack([tiles.T, tiles_before.T]),
        "dst_rows": np.concatenate([tiles_before[:, :1], tiles, tiles_behind[:, -1:]], axis=1),
        "dst_ends": np.stack([np.concatenate([before[:1], tiles[:, -1]]), np.concatenate([tiles[:, 0], behind[-1:]])]),
        "dst_flat": dst_p.reshape(1, NP),
        "et_flat": padded(edge_type_8, 0).reshape(1, NP),
        "nt_flat": padded(node_type_4, 0).reshape(NB, P, G).transpose(0, 2, 1).reshape(1, NP),
        "W": L0_gnn_W, "att_src": np.asarray(L0_gnn_att_src).reshape(1, P),
        "att_dst": np.asarray(L0_gnn_att_dst).reshape(1, P), "bias": np.asarray(L0_gnn_bias).reshape(1, P),
        "W_Q": L1_gnn_W_Q, "W_K": L1_gnn_W_K, "W_V": L1_gnn_W_V, "W_edge": L1_gnn_W_edge,
        "mu": np.asarray(L1_gnn_mu).reshape(1, ETYPES),
    }
    nc = bacc.Bacc("TRN2", target_bir_lowering=False, num_devices=1)
    given, d = {}, {}
    for name, a in arrays.items():
        a = np.ascontiguousarray(a)
        given[f"in_{name}"] = a
        dt = U32 if name == "edge_idx" else mybir.dt.from_np(a.dtype)
        d[name] = nc.dram_tensor(f"in_{name}", a.shape, dt, kind="ExternalInput").ap()
    d["out"] = nc.dram_tensor("out_0", (NP, P), F32, kind="ExternalOutput").ap()
    gnn(nc, d)
    r = run_bass_kernel_spmd(nc, [given], core_ids=[0])
    return r.results[0]["out_0"][:N]
```

```python
from contextlib import ExitStack

import concourse.bass as bass
from concourse import mybir

P = 128
N = 50000
G = 4
NT = 392
NP = NT * P
NB = NT // G
U = 4
ROWS = G * P
K = 4
Q = NT // K
HEADS = 4
NTYPES = 4
ETYPES = 8
LOW = NP // Q
BIG = 1.0e30
SPARE = 4 * ROWS
SKIP = float(1 << 20)

F32 = mybir.dt.float32
BF16 = mybir.dt.bfloat16
F16 = mybir.dt.float16
I32 = mybir.dt.int32
U32 = mybir.dt.uint32
F32R = mybir.dt.float32r
ALU = mybir.AluOpType
ACT = mybir.ActivationFunctionType
AX = mybir.AxisListType


class Batch:

    def __init__(self, m, c):
        self.m, self.c = m, c

    def slot(self, n):
        return self.c % n

    def turn(self, n):
        return self.m * (U // n) + self.c // n

    def before(self, n):
        return Batch(self.m, self.c - n)

    def at(self, size, offset=0):
        return self.m * (U * size) + (self.c * size + offset)


def staged(eng, *stages):
    last_lag = max(lag for lag, _ in stages)
    first = -(-(U + last_lag) // U) * U
    turns = NB // U

    def step(n):
        for lag, work in stages:
            if 0 <= n - lag < NB:
                work(Batch((n - lag) // U, (n - lag) % U))

    for n in range(first):
        step(n)
    with eng.Fori(first // U, turns) as m:
        for r in range(U):
            for lag, work in stages:
                back = (r - lag) // U
                work(Batch(m + back if back else m, (r - lag) % U))
    for n in range(turns * U, NB + last_lag):
        step(n)


def wait(eng, sems, batch, per=1, part=None, apart=None):
    if isinstance(batch.m, int) and U * batch.m + batch.c < 0:
        return
    n = len(sems)
    eng.wait_ge(sems[batch.slot(n)], batch.turn(n) * per + (per if part is None else part))
    if apart is not None:
        eng.sem_inc(apart, 1)


def all_landed(eng, sems, per):
    n = len(sems)
    for s in range(n):
        eng.wait_ge(sems[s], per * len(range(s, NB, n)))


def rows_of(table, row0, count=ROWS, g=G):
    return table[bass.ds(row0, count), :].rearrange("(p g) f -> p (g f)", g=g)


def parts_of(table, row0):
    return rows_of(table, row0).rearrange("p (g f) -> p g f", g=G)


def flat(tile):
    return tile[:, :, :].rearrange("p g f -> p (g f)")


def layer_norm_stats(dve, b, x, stats, mv, stat_done, mv_done, turns):
    for g in range(G):
        dve.bn_stats(stats[:, g, :], x[:, g, :]).then_inc(stat_done[0], 1)
    wait(dve, stat_done, b, G, apart=turns)
    for g in range(G):
        dve.bn_aggr(mv[:, g, :], stats[:, g, :]).then_inc(mv_done[0], 1)


def prepare(nc, sem, ident, d, keep):
    WX, WE, power, sidx = keep["WX"], keep["WE"], keep["power"], keep["sidx"]
    with ExitStack() as ctx:
        def sb(name, shape, dt=F32):
            return ctx.enter_context(nc.sbuf_tensor(name, shape, dt))

        ones = sb("ones", [P, P])
        att = sb("att", [P, 2, P])
        prod = sb("prod", [P, 2, P])
        mus = sb("mus", [P, ETYPES])
        wload = sb("wload", [P, ETYPES, P])
        wn = sb("wn", [P, NTYPES, 3 * P])
        dcol = sb("dcol", [P, NT], I32)
        dprev = sb("dprev", [P, NT], I32)
        same = sb("same", [P, NT])
        away = sb("away", [P, NT])
        spare = sb("spare", [P, -(-NT // (4 * G)) * 4 * G], I32)
        zero = sb("zero", [P, SPARE])
        drow = sb("drow", [Q, K, P + 2], I32)
        brow = sb("brow", [Q, K, P])
        w_ld, ones_set, id_set, prod_done = sem("w_ld"), sem("ones_set"), sem("id_set"), sem("prod_done")
        mus_done, same_done, brow_done, brow_st = sem("mus_done"), sem("same_done"), sem("brow_done"), sem("brow_st")
        prep_done, hi_done = sem("prep_done"), sem("hi_done")
        with nc.Block() as block:
            @block.sync
            def _(sp):
                sp.dma_start(WX[:, 0:P], d["W"][:, :]).then_inc(w_ld, 16)
                sp.dma_start(att[:, 0, :], d["att_src"].broadcast_to([P, P])).then_inc(w_ld, 16)
                sp.dma_start(att[:, 1, :], d["att_dst"].broadcast_to([P, P])).then_inc(w_ld, 16)
                sp.dma_start(mus[:, :], d["mu"].broadcast_to([P, ETYPES])).then_inc(w_ld, 16)
                sp.dma_start(wload[:, :, :], d["W_edge"].rearrange("t i o -> i t o")).then_inc(w_ld, 16)
                for i, name in enumerate(("W_Q", "W_K", "W_V")):
                    sp.dma_start(wn[:, :, i * P:(i + 1) * P],
                                 d[name].rearrange("t i o -> i t o")).then_inc(w_ld, 16)
                sp.dma_start(keep["bias"][:, :], d["bias"].broadcast_to([P, P])).then_inc(w_ld, 16)
                sp.dma_start(dcol[:, :], d["dst_cols"][0, :, :]).then_inc(w_ld, 16)
                sp.dma_start(dprev[:, :], d["dst_cols"][1, :, :]).then_inc(w_ld, 16)
                sp.dma_start(drow[:, :, :], d["dst_rows"].rearrange("(k q) e -> q k e", k=K)).then_inc(w_ld, 16)
                sp.wait_ge(brow_done, 1)
                sp.dma_start(d["brow"].rearrange("(k q) e -> q k e", k=K), brow[:, :, :]).then_inc(brow_st, 16)
                sp.wait_ge(id_set, 4)
                sp.dma_start(d["out"][NP:NP + SPARE, :].rearrange("(p r) f -> p (r f)", p=P), zero[:, :]).then_inc(brow_st, 16)
                sp.wait_ge(brow_st, 32)
                sp.wait_ge(w_ld, 16 * 12)

            @block.gpsimd
            def _(pool):
                pool.memset(ones[:, :], 1.0).then_inc(ones_set, 1)
                pool.wait_ge(ones_set, 1)
                pool.affine_select(out=ident[:, :], in_=ones[:, :], compare_op=ALU.is_equal, fill=0.0,
                                   base=0, pattern=[[-1, P]], channel_multiplier=1).then_inc(id_set, 1)
                pool.memset(power[:, :], -0.5).then_inc(id_set, 1)
                pool.iota(spare[:, :], pattern=[[0, -(-NT // (4 * G))], [P, 4 * G]], base=NP,
                          channel_multiplier=1).then_inc(id_set, 1)
                pool.memset(zero[:, :], 0.0).then_inc(id_set, 1)
                pool.wait_ge(id_set, 4)

            @block.vector
            def _(dve):
                dve.wait_ge(w_ld, 16 * 12)
                for i in range(2):
                    dve.tensor_tensor(prod[:, i, :], WX[:, 0:P], att[:, i, :], ALU.mult).then_inc(prod_done, 1)
                dve.wait_ge(prod_done, 2)
                dve.tensor_reduce(WX[:, P:P + 2 * HEADS], prod[:, :, :].rearrange("p i (h e) -> p (i h) e", h=HEADS),
                                  AX.X, ALU.add).then_inc(prep_done, 1)
                dve.tensor_copy(keep["WN_hi"][:, :, :], wn[:, :, :]).then_inc(hi_done, 1)
                dve.wait_ge(hi_done, 1)
                dve.tensor_tensor(keep["WN_lo"][:, :, :], wn[:, :, :], keep["WN_hi"][:, :, :],
                                  ALU.subtract).then_inc(prep_done, 1)
                dve.tensor_scalar(mus[:, :], mus[:, :], float(P) ** -0.5, None, ALU.mult).then_inc(mus_done, 1)
                dve.wait_ge(mus_done, 1)
                for t in range(ETYPES):
                    dve.tensor_scalar(WE[:, t, :], wload[:, t, :], mus[:, t:t + 1], None, ALU.mult).then_inc(prep_done, 1)
                dve.tensor_tensor(same[:, :], dcol[:, :], dprev[:, :], ALU.is_equal).then_inc(same_done, 1)
                dve.wait_ge(same_done, 1)
                dve.wait_ge(id_set, 4)
                dve.tensor_tensor(away[:, :], spare[:, 0:NT], dcol[:, :], ALU.subtract).then_inc(same_done, 1)
                dve.wait_ge(same_done, 2)
                dve.tensor_tensor(away[:, :], away[:, :], same[:, :], ALU.mult).then_inc(same_done, 1)
                dve.wait_ge(same_done, 3)
                dve.tensor_tensor(sidx[:, :], away[:, :], dcol[:, :], ALU.add).then_inc(prep_done, 1)
                dve.tensor_tensor(brow[:, :, :], drow[:, :, 1:P + 1],
                                  drow[:, :, P + 1:P + 2].broadcast_to([Q, K, P]), ALU.is_equal).then_inc(brow_done, 1)
                dve.wait_ge(prep_done, ETYPES + 3)


def count_edges(nc, one, d):
    with ExitStack() as ctx:
        def sb(n, name, shape, dt=F32):
            return [ctx.enter_context(nc.sbuf_tensor(f"c_{name}{s}", shape, dt)) for s in range(n)]

        dst, part_i, low_i = (sb(1, n, [P, NT], I32)[0] for n in ("dst", "part_i", "low_i"))
        part, low = sb(1, "part", [P, NT], F16)[0], sb(1, "low", [P, NT])[0]
        seq_i, seq = sb(1, "seq_i", [P, LOW], I32)[0], sb(1, "seq", [P, LOW], F16)[0]
        hot_part, hot_low = sb(2, "hot_part", [P, G, Q], BF16), sb(2, "hot_low", [P, G, LOW], BF16)
        ones, below = sb(1, "ones", [P, LOW])[0], sb(1, "below", [Q, Q])[0]
        zero = sb(1, "zero", [P, NP * 2 * HEADS // P])[0]
        cnt, upto, firsts, base, none = (sb(1, n, [Q, LOW])[0] for n in ("cnt", "upto", "firsts", "base", "none"))
        idx, idx0 = sb(1, "idx", [Q, LOW], U32)[0], sb(1, "idx0", [Q, LOW], U32)[0]
        ps = ctx.enter_context(nc.psum_tensor("c_ps", [P, LOW], F32))
        psB = ctx.enter_context(nc.psum_tensor("c_psB", [P, 512], F32))
        dst_ld, zero_st, idx_st = one("c_dst_ld")[0], one("c_zero_st")[0], one("c_idx_st")[0]
        consts, split, hot_done, counted, steps, based = (one(f"c_{n}") for n in (
            "consts", "split", "hot", "counted", "steps", "based"))
        with nc.Block() as block:
            @block.sync
            def _(sp):
                sp.dma_start(dst[:, :], d["dst_cols"][0, :, :]).then_inc(dst_ld, 16)
                sp.wait_ge(consts[0], 4)
                sp.dma_start(d["E0"][:, :].rearrange("(p r) f -> p (r f)", p=P), zero[:, :]).then_inc(zero_st, 16)
                sp.dma_start(d["T0"][NP:NP + 1, :], zero[0:1, 0:P + 2 * HEADS]).then_inc(zero_st, 16)
                sp.wait_ge(steps[0], 8)
                sp.dma_start(d["first_idx"].rearrange("(q r) g -> q (r g)", q=Q), idx[:, :]).then_inc(idx_st, 16)
                sp.dma_start(d["sums_idx"].rearrange("(q r) g -> q (r g)", q=Q), idx0[:, :]).then_inc(idx_st, 16)
                sp.wait_ge(zero_st, 32)
                sp.wait_ge(idx_st, 32)

            @block.gpsimd
            def _(pool):
                pool.iota(seq_i[:, :], pattern=[[1, LOW]], base=0, channel_multiplier=0).then_inc(consts[0], 1)
                pool.memset(ones[:, :], 1.0).then_inc(consts[0], 1)
                pool.memset(zero[:, :], 0.0).then_inc(consts[0], 1)
                pool.wait_ge(consts[0], 3)
                pool.affine_select(out=below[:, :], in_=ones[0:Q, 0:Q], compare_op=ALU.is_gt, fill=0.0, base=0,
                                   pattern=[[1, Q]], channel_multiplier=-1).then_inc(consts[0], 1)

            @block.vector
            def _(dve):
                dve.wait_ge(dst_ld, 16)
                dve.tensor_scalar(part_i[:, :], dst[:, :], LOW.bit_length() - 1, None,
                                  ALU.logical_shift_right).then_inc(split[0], 1)
                dve.tensor_scalar(low_i[:, :], dst[:, :], LOW - 1, None, ALU.bitwise_and).then_inc(split[0], 1)
                dve.wait_ge(split[0], 2)
                dve.tensor_copy(part[:, :], part_i[:, :]).then_inc(split[0], 1)
                dve.tensor_copy(low[:, :], low_i[:, :]).then_inc(split[0], 1)
                dve.wait_ge(consts[0], 4)
                dve.tensor_copy(seq[:, :], seq_i[:, :]).then_inc(split[0], 1)
                dve.wait_ge(split[0], 5)

                def one_hot(b):
                    wait(dve, counted, b.before(2))
                    dve.tensor_tensor(hot_part[b.slot(2)][:, :, :], seq[:, 0:Q].unsqueeze(1).broadcast_to([P, G, Q]),
                                      part[:, bass.ds(b.at(G), G)].unsqueeze(2).broadcast_to([P, G, Q]),
                                      ALU.is_equal).then_inc(hot_done[0], 1)
                    for g in range(G):
                        t = b.at(G, g)
                        dve.tensor_scalar(hot_low[b.slot(2)][:, g, :], seq[:, :], low[:, bass.ds(t, 1)], None,
                                          ALU.is_equal).then_inc(hot_done[0], 1)
                staged(dve, (0, one_hot))
                dve.wait_ge(counted[0], NB)
                dve.tensor_copy(cnt[:, :], ps[0:Q, :]).then_inc(steps[0], 1)
                dve.wait_ge(steps[0], 1)
                dve.tensor_tensor_scan(upto[:, :], ones[0:Q, :], cnt[:, :], 0.0, op0=ALU.mult, op1=ALU.add).then_inc(steps[0], 1)
                dve.tensor_scalar(none[:, :], cnt[:, :], 0.0, SKIP, ALU.is_equal, ALU.mult).then_inc(steps[0], 1)
                dve.wait_ge(steps[0], 3)
                dve.tensor_tensor(firsts[:, :], upto[:, :], cnt[:, :], ALU.subtract).then_inc(steps[0], 1)
                dve.wait_ge(based[0], 1)
                dve.tensor_copy(base[:, 0:1], psB[0:Q, 0:1]).then_inc(steps[0], 1)
                dve.wait_ge(steps[0], 5)
                dve.scalar_tensor_tensor(out=upto[:, :], in0=firsts[:, :], scalar=base[:, 0:1], in1=none[:, :],
                                         op0=ALU.add, op1=ALU.add).then_inc(steps[0], 1)
                dve.wait_ge(steps[0], 6)
                dve.tensor_copy(idx[:, :], upto[:, :]).then_inc(steps[0], 1)
                dve.tensor_scalar(idx0[:, :], upto[:, :], float(NP), None, ALU.min).then_inc(steps[0], 1)

            @block.tensor
            def _(pe):
                def count(b):
                    number = U * b.m + b.c if isinstance(b.m, int) else None
                    for g in range(G):
                        wait(pe, hot_done, b, 1 + G, g + 2)
                        mm = pe.matmul(ps[0:Q, :], hot_part[b.slot(2)][:, g, :], hot_low[b.slot(2)][:, g, :],
                                       start=(number == 0 and g == 0), stop=(number == NB - 1 and g == G - 1))
                    mm.then_inc(counted[0], 1)
                staged(pe, (0, count))
                pe.wait_ge(steps[0], 3)
                pe.wait_ge(consts[0], 4)
                pe.matmul(psB[0:Q, 0:1], below[:, :], upto[:, LOW - 1:LOW], start=True, stop=True).then_inc(based[0], 1)


def project_nodes(nc, one, ring, ident, d, keep):
    WX = keep["WX"]
    HA = P + HEADS
    with ExitStack() as ctx:
        def sb(n, name, shape, dt=F32):
            return [ctx.enter_context(nc.sbuf_tensor(f"n0_{name}{s}", shape, dt)) for s in range(n)]

        x, h, hT, rows = sb(4, "x", [P, G, P]), sb(2, "h", [P, G, P]), sb(2, "hT", [P, ROWS]), sb(4, "rows", [P, G, HA + HEADS])
        stats, mv = sb(4, "stats", [P, G, 6]), sb(4, "mv", [P, G, 2])
        rstd, nmr = sb(4, "rstd", [P, 2, G]), sb(4, "nmr", [P, 2, G])
        idx = sb(4, "idx", [P, G], U32)
        ad, drows = sb(4, "ad", [P, G, HEADS]), sb(4, "drows", [P, G, 2 * HEADS])
        psT = [ctx.enter_context(nc.psum_tensor(f"n0_psT{s}", [P, ROWS], F32)) for s in range(2)]
        psH = [ctx.enter_context(nc.psum_tensor(f"n0_psH{s}", [P, G, 256], F32)) for s in range(2)]
        x_ld, rows_st, drows_st, idx_ld = (ring("n0_x_ld", 4), ring("n0_rows_st", 4), ring("n0_drows_st", 4),
                                           ring("n0_idx_ld", 4))
        stat_done, mv_done, nmr_done = one("n0_stat"), one("n0_mv"), one("n0_nmr")
        var_done, root_done, rstd_done = one("n0_var"), one("n0_root"), one("n0_rstd")
        h_done, t_done, hT_done, mm_done = one("n0_h"), one("n0_t"), one("n0_hT"), one("n0_mm")
        rows_done, ad_done, drows_done, turns = one("n0_rows"), one("n0_ad"), one("n0_drows"), one("n0_turns")[0]
        with nc.Block() as block:
            @block.sync
            def _(sp):
                def load(b):
                    wait(sp, h_done, b.before(4), G)
                    sp.dma_start(flat(x[b.slot(4)]), rows_of(d["x"], b.at(ROWS))).then_inc(x_ld[b.slot(4)], 16)

                def load_idx(b):
                    wait(sp, drows_st, b.before(4), 16 * G)
                    sp.dma_start(idx[b.slot(4)][:, :], rows_of(d["first_idx"], b.at(P), P, 1)).then_inc(idx_ld[b.slot(4)], 16)
                staged(sp, (0, load), (3, load_idx))

            @block.vector
            def _(dve):
                def moments(b):
                    wait(dve, x_ld, b, 16, apart=turns)
                    wait(dve, nmr_done, b.before(4), apart=turns)
                    layer_norm_stats(dve, b, x[b.slot(4)], stats[b.slot(4)], mv[b.slot(4)], stat_done, mv_done, turns)
                    wait(dve, mv_done, b, G)
                    dve.tensor_scalar(rstd[b.slot(4)][:, 0, :], mv[b.slot(4)][:, :, 1], 1e-5, None,
                                      ALU.add).then_inc(var_done[0], 1)

                def scale(b):
                    four = b.slot(4)
                    wait(dve, root_done, b, apart=turns)
                    wait(dve, h_done, b.before(4), G, apart=turns)
                    dve.reciprocal(rstd[four][:, 1, :], nmr[four][:, 0, :]).then_inc(rstd_done[0], 1)
                    wait(dve, rstd_done, b)
                    dve.scalar_tensor_tensor(out=nmr[four][:, 1, :], in0=mv[four][:, :, 0], scalar=-1.0,
                                             in1=rstd[four][:, 1, :], op0=ALU.mult, op1=ALU.mult).then_inc(nmr_done[0], 1)

                def turned(b):
                    wait(dve, t_done, b)
                    wait(dve, mm_done, b.before(2))
                    dve.tensor_copy(hT[b.slot(2)][:, :], psT[b.slot(2)][:, :]).then_inc(hT_done[0], 1)

                def self_scores(b):
                    r, a, dr = rows[b.slot(4)], ad[b.slot(4)], drows[b.slot(4)]
                    wait(dve, rows_done, b)
                    wait(dve, drows_st, b.before(4), 16 * G)
                    dve.tensor_copy(dr[:, :, 0:HEADS], r[:, :, HA:HA + HEADS]).then_inc(ad_done[0], 1)
                    dve.tensor_tensor(a[:, :, :], r[:, :, P:HA], r[:, :, HA:HA + HEADS], ALU.add).then_inc(ad_done[0], 1)
                    wait(dve, ad_done, b, 2)
                    dve.scalar_tensor_tensor(out=dr[:, :, HEADS:2 * HEADS], in0=a[:, :, :], scalar=0.2,
                                             in1=a[:, :, :], op0=ALU.mult, op1=ALU.max).then_inc(drows_done[0], 1)
                staged(dve, (0, moments), (1, scale), (2, turned), (4, self_scores))

            @block.gpsimd
            def _(pool):
                def scatter(b):
                    wait(pool, idx_ld, b, 16, apart=turns)
                    wait(pool, drows_done, b, apart=turns)
                    for g in range(G):
                        pool.indirect_dma_start(d["E0"][:, :], bass.IndirectOffsetOnAxis(ap=idx[b.slot(4)][:, g:g + 1], axis=0),
                                                drows[b.slot(4)][:, g, :], None, bounds_check=NP - 1,
                                                oob_is_err=False).then_inc(drows_st[b.slot(4)], 16)
                staged(pool, (0, scatter))
                all_landed(pool, drows_st, 16 * G)

            @block.scalar
            def _(act):
                def root(b):
                    wait(act, var_done, b)
                    act.activation(nmr[b.slot(4)][:, 0, :], rstd[b.slot(4)][:, 0, :], ACT.Sqrt).then_inc(root_done[0], 1)

                def normalise(b):
                    wait(act, nmr_done, b)
                    wait(act, t_done, b.before(2))
                    for g in range(G):
                        act.activation(h[b.slot(2)][:, g, :], x[b.slot(4)][:, g, :], ACT.Relu,
                                       bias=nmr[b.slot(4)][:, 1, g:g + 1],
                                       scale=rstd[b.slot(4)][:, 1, g:g + 1]).then_inc(h_done[0], 1)

                def products(b):
                    wait(act, mm_done, b)
                    wait(act, rows_st, b.before(4), 16)
                    wait(act, drows_done, b.before(4))
                    act.activation(rows[b.slot(4)][:, :, :], psH[b.slot(2)][:, :, 0:HA + HEADS],
                                   ACT.Copy).then_inc(rows_done[0], 1)
                    wait(act, rows_done, b)
                    act.dma_start(parts_of(d["HA"], b.at(ROWS)), rows[b.slot(4)][:, :, 0:HA]).then_inc(rows_st[b.slot(4)], 16)
                staged(act, (0, root), (1, normalise), (3, products))
                all_landed(act, rows_st, 16)

            @block.tensor
            def _(pe):
                def turn(b):
                    wait(pe, hT_done, b.before(2))
                    for g in range(G):
                        wait(pe, h_done, b, G, g + 1)
                        mm = pe.transpose(psT[b.slot(2)][:, g * P:(g + 1) * P], h[b.slot(2)][:, g, :], ident[:, :])
                    mm.then_inc(t_done[0], 1)

                def project(b):
                    wait(pe, hT_done, b)
                    wait(pe, rows_done, b.before(2))
                    for g in range(G):
                        mm = pe.matmul(psH[b.slot(2)][:, g, 0:P + 2 * HEADS], hT[b.slot(2)][:, g * P:(g + 1) * P],
                                       WX[:, :], start=True, stop=True)
                    mm.then_inc(mm_done[0], 1)
                staged(pe, (0, turn), (1, project))


def gather_scores_0(nc, one, ring, d, keep):
    SC = keep["SC"]
    HA = P + HEADS
    with ExitStack() as ctx:
        def sb(n, name, shape, dt=F32):
            return [ctx.enter_context(nc.sbuf_tensor(f"a0_{name}{s}", shape, dt)) for s in range(n)]

        idx, srow = sb(4, "idx", [P, 2 * G], U32), sb(4, "srow", [P, G, HA])
        idx_ld, gathered, msg_st = ring("a0_idx_ld", 4), ring("a0_gathered", 4), ring("a0_msg_st", 4)
        sc_done, turns = one("a0_sc"), one("a0_turns")[0]
        with nc.Block() as block:
            @block.sync
            def _(sp):
                def load(b):
                    wait(sp, gathered, b.before(4), 16 * G)
                    sp.dma_start(idx[b.slot(4)][:, :], rows_of(d["edge_idx"], b.at(P), P, 1)).then_inc(idx_ld[b.slot(4)], 16)
                staged(sp, (0, load))

            @block.scalar
            def _(act):
                def store(b):
                    wait(act, gathered, b, 16 * G)
                    act.dma_start(parts_of(d["M"], b.at(ROWS)), srow[b.slot(4)][:, :, 0:P]).then_inc(msg_st[b.slot(4)], 16)
                staged(act, (0, store))
                all_landed(act, msg_st, 16)

            @block.gpsimd
            def _(pool):
                def gather(b):
                    i = idx[b.slot(4)]
                    wait(pool, idx_ld, b, 16, apart=turns)
                    wait(pool, msg_st, b.before(4), 16, apart=turns)
                    wait(pool, sc_done, b.before(4), apart=turns)
                    for g in range(G):
                        pool.indirect_dma_start(srow[b.slot(4)][:, g, :], None, d["HA"][:, :], bass.IndirectOffsetOnAxis(
                            ap=i[:, g:g + 1], axis=0)).then_inc(gathered[b.slot(4)], 16)
                staged(pool, (0, gather))

            @block.vector
            def _(dve):
                def score(b):
                    wait(dve, gathered, b, 16 * G)
                    dve.tensor_copy(SC[:, :, bass.ds(b.at(G), G)].rearrange("p h g -> p g h"),
                                    srow[b.slot(4)][:, :, P:HA]).then_inc(sc_done[0], 1)
                staged(dve, (0, score))


def segment_softmax(nc, sem, ident, d, H, SC, SE, least, tag):
    C = 2 * H
    with ExitStack() as ctx:
        def sb(name, shape, dt=F32):
            return ctx.enter_context(nc.sbuf_tensor(f"{tag}_{name}", shape, dt))

        drow = sb("drow", [Q, K, P + 2], I32)
        ends = sb("ends", [C, 2, NT + 1], I32)
        far = sb("far", [Q, 2, K, P])
        tile_far = sb("tile_far", [C, 2, NT])
        row = sb("row", [Q, K, H, P])
        top = sb("top", [Q, K, H, P])
        scan = [sb(f"scan{i}", [Q, K, H, P]) for i in range(2)]
        tile_end = sb("tile_end", [H, 2, NT])
        carry = sb("carry", [H, 2, NT + 1])
        carry_in = sb("carry_in", [Q, 2, K * H])
        if SE is not None:
            erow, fill = sb("erow", [Q, K, P, C]), sb("fill", [Q, K, C, P])
            same, tile_same = sb("same", [Q, K, P]), sb("tile_same", [C, NT])
            fill_end, fill_carry, fill_in = sb("fill_end", [C, NT]), sb("fill_carry", [C, NT + 1]), sb("fill_in", [Q, K * C])
        ps = [ctx.enter_context(nc.psum_tensor(f"{tag}_ps{i}", [P, 512], F32)) for i in range(8)]
        names = ("ld", "flag", "far", "turned", "row", "fill", "fend_t", "fend", "fcarry", "fin_t", "fin", "fill2",
                 "sum", "leaky", "top", "scan", "end_t", "end", "carry", "in_t", "in", "scan2", "max", "least", "sub",
                 "exp", "back", "out")
        S = {n: sem(f"{tag}_{n}") for n in names}
        with nc.Block() as block:
            @block.sync
            def _(sp):
                sp.dma_start(drow[:, :, :], d["dst_rows"].rearrange("(k q) e -> q k e", k=K)).then_inc(S["ld"], 16)
                for i in range(2):
                    sp.dma_start(ends[:, i, :], d["dst_ends"][i:i + 1, :].broadcast_to([C, NT + 1])).then_inc(S["ld"], 16)
                if SE is not None:
                    sp.dma_start(erow[:, :, :, :].rearrange("q k e c -> q k (e c)"),
                                 d["E0"].rearrange("(k q e) c -> q k (e c)", k=K, e=P)).then_inc(S["ld"], 16)
                sp.wait_ge(S["ld"], 48 if SE is None else 64)

            @block.vector
            def _(dve):
                dve.wait_ge(S["ld"], 48 if SE is None else 64)
                for i in range(2):
                    dve.tensor_tensor(far[:, i, :, :], drow[:, :, 1:P + 1], drow[:, :, 2 * i:2 * i + P],
                                      ALU.not_equal).then_inc(S["flag"], 1)
                    dve.tensor_tensor(tile_far[:, i, :], ends[:, i, 1:NT + 1], ends[:, i, 0:NT],
                                      ALU.not_equal).then_inc(S["flag"], 1)
                dve.memset(carry[:, 0, 0:1], -BIG).then_inc(S["flag"], 1)
                dve.memset(carry[:, 1, NT:NT + 1], -BIG).then_inc(S["flag"], 1)
                if SE is not None:
                    dve.tensor_tensor(same[:, :, :], drow[:, :, 1:P + 1], drow[:, :, 0:P], ALU.is_equal).then_inc(S["flag"], 1)
                    dve.tensor_tensor(tile_same[:, :], ends[:, 0, 1:NT + 1], ends[:, 0, 0:NT],
                                      ALU.is_equal).then_inc(S["flag"], 1)
                    dve.memset(fill_carry[:, 0:1], 0.0).then_inc(S["flag"], 1)
                dve.wait_ge(S["flag"], 6 if SE is None else 9)
                dve.tensor_scalar(far[:, :, :, :], far[:, :, :, :], -BIG, None, ALU.mult).then_inc(S["far"], 1)
                dve.tensor_scalar(tile_far[:, :, :], tile_far[:, :, :], -BIG, None, ALU.mult).then_inc(S["far"], 1)
                dve.wait_ge(S["far"], 2)
                if SE is not None:
                    for k in range(K):
                        for c in range(C):
                            dve.tensor_tensor_scan(fill[:, k, c, :], same[:, k, :], erow[:, k, :, c], 0.0, op0=ALU.mult,
                                                   op1=ALU.add).then_inc(S["fill"], 1)
                    dve.wait_ge(S["fend"], 1)
                    dve.tensor_tensor_scan(fill_carry[:, 1:NT + 1], tile_same[:, :], fill_end[:, :], 0.0, op0=ALU.mult,
                                           op1=ALU.add).then_inc(S["fcarry"], 1)
                    dve.wait_ge(S["fin"], 1)
                    for k in range(K):
                        for c in range(C):
                            dve.tensor_tensor_scan(fill[:, k, c, :], same[:, k, :], erow[:, k, :, c],
                                                   fill_in[:, k * C + c:k * C + c + 1], op0=ALU.mult,
                                                   op1=ALU.add).then_inc(S["fill2"], 1)
                    dve.wait_ge(S["fill2"], K * C)
                    dve.wait_ge(S["row"], K)
                    dve.tensor_tensor(row[:, :, :, :], row[:, :, :, :], fill[:, :, 0:H, :], ALU.add).then_inc(S["sum"], 1)
                    dve.wait_ge(S["sum"], 1)
                    dve.scalar_tensor_tensor(out=row[:, :, :, :], in0=row[:, :, :, :], scalar=0.2, in1=row[:, :, :, :],
                                             op0=ALU.mult, op1=ALU.max).then_inc(S["leaky"], 1)
                    dve.wait_ge(S["leaky"], 1)
                    dve.tensor_tensor(top[:, :, :, :], row[:, :, :, :], fill[:, :, H:C, :], ALU.max).then_inc(S["top"], 1)
                else:
                    dve.wait_ge(S["row"], K)
                    dve.tensor_copy(top[:, :, :, :], row[:, :, :, :]).then_inc(S["top"], 1)
                dve.wait_ge(S["top"], 1)

                def scans(k, h, start):
                    a, b, o = far[:, :, k, :], top[:, k, h, :], [scan[i][:, k, h, :] for i in range(2)]
                    one = dve.tensor_tensor_scan(o[0], a[:, 0, :], b, start[0], op0=ALU.add, op1=ALU.max)
                    two = dve.tensor_tensor_scan(o[1][:, ::-1], a[:, 1, ::-1], b[:, ::-1], start[1], op0=ALU.add,
                                                 op1=ALU.max)
                    return one, two

                for k in range(K):
                    for h in range(H):
                        for ins in scans(k, h, (-BIG, -BIG)):
                            ins.then_inc(S["scan"], 1)
                dve.wait_ge(S["end"], 2)
                dve.tensor_tensor_scan(carry[:, 0, 1:NT + 1], tile_far[0:H, 0, :], tile_end[:, 0, :], -BIG, op0=ALU.add,
                                       op1=ALU.max).then_inc(S["carry"], 1)
                dve.tensor_tensor_scan(carry[:, 1, 0:NT][:, ::-1], tile_far[0:H, 1, ::-1], tile_end[:, 1, ::-1], -BIG,
                                       op0=ALU.add, op1=ALU.max).then_inc(S["carry"], 1)
                dve.wait_ge(S["in"], 1)
                for k in range(K):
                    for h in range(H):
                        c = k * H + h
                        for ins in scans(k, h, (carry_in[:, 0, c:c + 1], carry_in[:, 1, c:c + 1])):
                            ins.then_inc(S["scan2"], 1)
                dve.wait_ge(S["scan2"], 2 * K * H)
                dve.tensor_tensor(top[:, :, :, :], scan[0][:, :, :, :], scan[1][:, :, :, :], ALU.max).then_inc(S["max"], 1)
                dve.wait_ge(S["max"], 1)
                if least is not None:
                    dve.tensor_scalar(top[:, :, :, :], top[:, :, :, :], least, None, ALU.max).then_inc(S["least"], 1)
                    dve.wait_ge(S["least"], 1)
                dve.tensor_tensor(row[:, :, :, :], row[:, :, :, :], top[:, :, :, :], ALU.subtract).then_inc(S["sub"], 1)
                if SE is not None:
                    dve.tensor_tensor(fill[:, :, H:C, :], fill[:, :, H:C, :], top[:, :, :, :],
                                      ALU.subtract).then_inc(S["sub"], 1)

            @block.tensor
            def _(pe):
                for k in range(K):
                    for h in range(H):
                        mm = pe.transpose(ps[k][0:Q, h * P:(h + 1) * P], SC[:, h, k * Q:(k + 1) * Q], ident[:, :])
                    mm.then_inc(S["turned"], 1)
                if SE is not None:
                    pe.wait_ge(S["fill"], K * C)
                    for k in range(K):
                        mm = pe.transpose(ps[4][0:C, k * Q:(k + 1) * Q], fill[:, k, :, P - 1], ident[0:Q, 0:Q])
                    mm.then_inc(S["fend_t"], 1)
                    pe.wait_ge(S["fcarry"], 1)
                    for k in range(K):
                        mm = pe.transpose(ps[5][0:Q, k * C:(k + 1) * C], fill_carry[:, k * Q:(k + 1) * Q], ident[0:C, 0:C])
                    mm.then_inc(S["fin_t"], 1)
                pe.wait_ge(S["scan"], 2 * K * H)
                if SE is not None:
                    pe.wait_ge(S["fin"], 1)
                for i in range(2):
                    for k in range(K):
                        mm = pe.transpose(ps[4 + i][0:H, k * Q:(k + 1) * Q], scan[i][:, k, :, (1 - i) * (P - 1)],
                                          ident[0:Q, 0:Q])
                    mm.then_inc(S["end_t"], 1)
                pe.wait_ge(S["carry"], 2)
                for i in range(2):
                    for k in range(K):
                        mm = pe.transpose(ps[6][0:Q, (i * K + k) * H:(i * K + k + 1) * H],
                                          carry[:, i, k * Q + i:(k + 1) * Q + i], ident[0:H, 0:H])
                mm.then_inc(S["in_t"], 1)
                pe.wait_ge(S["exp"], 1)
                pe.wait_ge(S["in"], 1)
                for h in range(H):
                    for k in range(K):
                        mm = pe.transpose(ps[h][:, k * Q:(k + 1) * Q], row[:, k, h, :], ident[0:Q, 0:Q])
                    mm.then_inc(S["back"], 1)
                if SE is not None:
                    pe.wait_ge(S["exp"], 2)
                    for h in range(H):
                        for k in range(K):
                            mm = pe.transpose(ps[H + h][:, k * Q:(k + 1) * Q], fill[:, k, H + h, :], ident[0:Q, 0:Q])
                        mm.then_inc(S["back"], 1)

            @block.scalar
            def _(act):
                for k in range(K):
                    act.wait_ge(S["turned"], k + 1)
                    act.activation(row[:, k, :, :].rearrange("q h e -> q (h e)"), ps[k][0:Q, 0:H * P],
                                   ACT.Copy).then_inc(S["row"], 1)
                if SE is not None:
                    act.wait_ge(S["fend_t"], 1)
                    act.activation(fill_end[:, :], ps[4][0:C, 0:NT], ACT.Copy).then_inc(S["fend"], 1)
                    act.wait_ge(S["fin_t"], 1)
                    act.activation(fill_in[:, :], ps[5][0:Q, 0:K * C], ACT.Copy).then_inc(S["fin"], 1)
                for i in range(2):
                    act.wait_ge(S["end_t"], i + 1)
                    act.activation(tile_end[:, i, :], ps[4 + i][0:H, 0:NT], ACT.Copy).then_inc(S["end"], 1)
                act.wait_ge(S["in_t"], 1)
                act.activation(carry_in[:, :, :].rearrange("q i c -> q (i c)"), ps[6][0:Q, 0:2 * K * H],
                               ACT.Copy).then_inc(S["in"], 1)
                act.wait_ge(S["sub"], 1)
                act.activation(row[:, :, :, :], row[:, :, :, :], ACT.Exp).then_inc(S["exp"], 1)
                if SE is not None:
                    act.wait_ge(S["sub"], 2)
                    act.activation(fill[:, :, H:C, :], fill[:, :, H:C, :], ACT.Exp).then_inc(S["exp"], 1)
                banks = [(SC, h) for h in range(H)] + ([(SE, h) for h in range(H)] if SE is not None else [])
                for n, (to, h) in enumerate(banks):
                    act.wait_ge(S["back"], n + 1)
                    act.activation(to[:, h, :], ps[n][:, 0:NT], ACT.Copy).then_inc(S["out"], 1)
                act.wait_ge(S["out"], len(banks))


def segment_sums(nc, one, ring, d, keep, H, EX, WS, table, tag):
    W = P + H
    WT = W + (H if WS is not None else 0)
    C = P // H
    by_edge = WS is not None
    outs = G + (1 if by_edge else 0)
    writes = 1 if by_edge else G
    with ExitStack() as ctx:
        def sb(n, name, shape, dt=F32):
            return [ctx.enter_context(nc.sbuf_tensor(f"{tag}_{name}{s}", shape, dt)) for s in range(n)]

        m, drow, brow = sb(4, "m", [P, G, P]), sb(4, "drow", [P, G, P], I32), sb(4, "brow", [1, ROWS])
        adj, msg, carry = sb(2, "adj", [P, G, P]), sb(2, "msg", [P, G, W]), sb(4, "carry", [1, G, W])
        out, idx, dcol = sb(4, "out", [P, G, WT]), sb(4, "idx", [P, G], U32), sb(1, "dcol", [P, NT], I32)[0]
        dn, mean = sb(2, "dn", [P, 2, G]), sb(4, "mean", [P, G, P])
        ps = [[ctx.enter_context(nc.psum_tensor(f"{tag}_ps{s}{g}", [P, 512], F32)) for g in range(G)] for s in range(2)]
        ld, scat = ring(f"{tag}_ld", 4), ring(f"{tag}_scat", 4)
        msg_done, adj_done, idx_done, own_done = one(f"{tag}_msg"), one(f"{tag}_adj"), one(f"{tag}_idx"), one(f"{tag}_own")
        dn_done, mean_done = one(f"{tag}_dn"), one(f"{tag}_mean")
        sum_done, carry_done, out_done = one(f"{tag}_sum"), one(f"{tag}_carry"), one(f"{tag}_out")
        dcol_ld, zero_set, turns = one(f"{tag}_dcol_ld")[0], one(f"{tag}_zero")[0], one(f"{tag}_turns")[0]
        LAST = NT - G
        with nc.Block() as block:
            @block.sync
            def _(sp):
                sp.dma_start(dcol[:, :], d["dst_cols"][0, :, :]).then_inc(dcol_ld, 16)

                def store(b):
                    wait(sp, out_done, b, outs)
                    sp.dma_start(table[bass.ds(b.at(-ROWS, LAST * P), ROWS), :].rearrange("(g p) f -> p g f", g=G),
                                 out[b.slot(4)][:, :, :]).then_inc(scat[b.slot(4)], 16)

                def load(b):
                    s, row0 = b.slot(4), b.at(-ROWS, LAST * P)
                    wait(sp, msg_done, b.before(4), 2, apart=turns)
                    wait(sp, adj_done, b.before(4), apart=turns)
                    wait(sp, sum_done, b.before(4), G, apart=turns)
                    sp.dma_start(flat(m[s]), rows_of(d["M"], row0)).then_inc(ld[s], 16)
                    sp.dma_start(flat(drow[s]), d["dst_flat"][0:1, bass.ds(row0, ROWS)].broadcast_to([P, ROWS])).then_inc(ld[s], 16)
                    sp.dma_start(brow[s][:, :], d["brow_flat"][0:1, bass.ds(row0, ROWS)]).then_inc(ld[s], 16)
                if by_edge:
                    staged(sp, (0, load), (3, store))
                    all_landed(sp, scat, 16)
                else:
                    staged(sp, (0, load))

            @block.vector
            def _(dve):
                dve.memset(carry[3][:, 0, :], 0.0).then_inc(zero_set, 1)
                dve.wait_ge(dcol_ld, 16)

                def weigh(b):
                    tiles = bass.ds(b.at(-G, LAST), G)
                    loaded, ad, ms = m[b.slot(4)], adj[b.slot(2)], msg[b.slot(2)]
                    wait(dve, ld, b, 48)
                    wait(dve, own_done, b.before(2))
                    dve.tensor_tensor(ad[:, :, :], drow[b.slot(4)][:, :, :],
                                      dcol[:, tiles].unsqueeze(2).broadcast_to([P, G, P]), ALU.is_equal).then_inc(adj_done[0], 1)
                    ex = EX[:, :, tiles].rearrange("p h g -> p g h")
                    if H > 1:
                        dve.tensor_tensor(ms[:, :, 0:P].rearrange("p g (h c) -> p g h c", h=H),
                                          loaded[:, :, :].rearrange("p g (h c) -> p g h c", h=H),
                                          ex.unsqueeze(3).broadcast_to([P, G, H, C]), ALU.mult).then_inc(msg_done[0], 1)
                    else:
                        dve.tensor_tensor(ms[:, :, 0:P], loaded[:, :, :], ex.broadcast_to([P, G, P]),
                                          ALU.mult).then_inc(msg_done[0], 1)
                    dve.tensor_copy(ms[:, :, P:W], ex).then_inc(msg_done[0], 1)

                def hand_on(b):
                    wait(dve, own_done, b, apart=turns)
                    wait(dve, ld, b, 48, apart=turns)
                    wait(dve, sum_done, b.before(3), G, apart=turns)
                    for g in reversed(range(G)):
                        incoming = carry[b.slot(4)][:, g + 1, :] if g < G - 1 else carry[b.before(1).slot(4)][:, 0, :]
                        if g < G - 1:
                            wait(dve, carry_done, b, G, G - 1 - g)
                        else:
                            wait(dve, carry_done, b.before(1), G)
                        dve.scalar_tensor_tensor(out=carry[b.slot(4)][:, g, :], in0=incoming,
                                                 scalar=brow[b.slot(4)][:, g * P:g * P + 1],
                                                 in1=ps[b.slot(2)][g][0:1, 0:W], op0=ALU.mult,
                                                 op1=ALU.add).then_inc(carry_done[0], 1)

                def divide(b):
                    o, n = out[b.slot(4)], dn[b.slot(2)]
                    wait(dve, out_done, b, outs)
                    dve.tensor_scalar(n[:, 0, :], o[:, :, P], 1e-10, None, ALU.add).then_inc(dn_done[0], 1)
                    wait(dve, dn_done, b, 2, 1)
                    dve.reciprocal(n[:, 1, :], n[:, 0, :]).then_inc(dn_done[0], 1)
                    wait(dve, dn_done, b, 2)
                    wait(dve, scat, b.before(4), 16 * writes)
                    dve.tensor_copy(idx[b.slot(4)][:, :], keep["sidx"][:, bass.ds(b.at(-G, LAST), G)]).then_inc(idx_done[0], 1)
                    dve.tensor_tensor(mean[b.slot(4)][:, :, :], o[:, :, 0:P],
                                      n[:, 1, :].unsqueeze(2).broadcast_to([P, G, P]), ALU.mult).then_inc(mean_done[0], 1)
                if by_edge:
                    staged(dve, (0, weigh), (1, hand_on))
                else:
                    staged(dve, (0, weigh), (1, hand_on), (2, divide))

            @block.tensor
            def _(pe):
                pe.wait_ge(zero_set, 1)

                def own(b):
                    wait(pe, msg_done, b, 2)
                    wait(pe, adj_done, b)
                    for g in reversed(range(G)):
                        wait(pe, out_done, b.before(2), outs, outs - g)
                        mm = pe.matmul(ps[b.slot(2)][g][:, 0:W], adj[b.slot(2)][:, g, :], msg[b.slot(2)][:, g, :],
                                       start=True, stop=True)
                    mm.then_inc(own_done[0], 1)

                def behind(b):
                    wait(pe, carry_done, b, G)
                    for g in reversed(range(G)):
                        row = carry[b.slot(4)][:, g + 1, :] if g < G - 1 else carry[b.before(1).slot(4)][:, 0, :]
                        pe.matmul(ps[b.slot(2)][g][:, 0:W], brow[b.slot(4)][:, g * P:(g + 1) * P], row, start=False,
                                  stop=True, skip_group_check=True).then_inc(sum_done[0], 1)
                staged(pe, (0, own), (1, behind))

            @block.scalar
            def _(act):
                def take(b):
                    o = out[b.slot(4)]
                    if by_edge:
                        wait(act, scat, b.before(4), 16)
                    else:
                        wait(act, mean_done, b.before(4))
                    if WS is not None:
                        act.activation(o[:, :, W:WT], WS[:, :, bass.ds(b.at(-G, LAST), G)].rearrange("p h g -> p g h"),
                                       ACT.Copy).then_inc(out_done[0], 1)
                    for g in reversed(range(G)):
                        wait(act, sum_done, b, G, G - g)
                        act.activation(o[:, g, 0:W], ps[b.slot(2)][g][:, 0:W], ACT.Copy).then_inc(out_done[0], 1)
                staged(act, (0, take))

            @block.gpsimd
            def _(pool):
                def scatter(b):
                    wait(pool, idx_done, b, apart=turns)
                    wait(pool, mean_done, b, apart=turns)
                    for g in reversed(range(G)):
                        pool.indirect_dma_start(table[:, :], bass.IndirectOffsetOnAxis(ap=idx[b.slot(4)][:, g:g + 1], axis=0),
                                                mean[b.slot(4)][:, g, :], None, compute_op=ALU.add).then_inc(
                                                    scat[b.slot(4)], 16)
                if not by_edge:
                    staged(pool, (0, scatter))
                    all_landed(pool, scat, 16 * writes)


def finish_0_project_1(nc, one, ring, ident, d, keep):
    HA = P + HEADS
    WT = P + 2 * HEADS
    C = P // HEADS
    with ExitStack() as ctx:
        def sb(n, name, shape, dt=F32):
            return [ctx.enter_context(nc.sbuf_tensor(f"n1_{name}{s}", shape, dt)) for s in range(n)]

        x, ha, t0, nt = sb(4, "x", [P, G, P]), sb(4, "ha", [P, G, HA]), sb(4, "t0", [P, G, WT]), sb(4, "nt", [P, ROWS], I32)
        tot, w, dn, r = (sb(2, n, [P, G, HEADS]) for n in ("tot", "w", "dn", "r"))
        u, e, x1, h = sb(2, "u", [P, G, P]), sb(2, "e", [P, G, P]), sb(4, "x1", [P, G, P]), sb(2, "h", [P, G, P])
        stats, mv = sb(4, "stats", [P, G, 6]), sb(4, "mv", [P, G, 2])
        rstd, nmr = sb(4, "rstd", [P, 2, G]), sb(4, "nmr", [P, 2, G])
        hTm, hi, lo = sb(2, "hTm", [P, NTYPES, ROWS]), sb(4, "hi", [P, NTYPES, ROWS], F32R), sb(4, "lo", [P, NTYPES, ROWS], F32R)
        qkv = sb(4, "qkv", [P, G, 3 * P])
        psT = [ctx.enter_context(nc.psum_tensor(f"n1_psT{s}", [P, ROWS], F32)) for s in range(2)]
        psQ = [ctx.enter_context(nc.psum_tensor(f"n1_psQ{g}", [P, 512], F32)) for g in range(G)]
        idx = sb(4, "idx", [P, G], U32)
        ld, x1_st, qkv_st = ring("n1_ld", 4), ring("n1_x1_st", 4), ring("n1_qkv_st", 4)
        idx_ld, nt_ld, gathered = ring("n1_idx_ld", 4), ring("n1_nt_ld", 4), ring("n1_gathered", 4)
        small, wide, below_done, exp_done, x1_done = (one(f"n1_{n}") for n in ("small", "wide", "below", "exp", "x1"))
        stat_done, mv_done, var_done, rstd_done, nmr_done = (one(f"n1_{n}") for n in ("stat", "mv", "var", "rstd", "nmr"))
        h_done, t_done, hT_done, mm_done = one("n1_h"), one("n1_t"), one("n1_hT"), one("n1_mm")
        xu_done, qkv_done, turns = one("n1_xu"), one("n1_qkv"), one("n1_turns")[0]
        hi_done, pool_lo_done, dve_lo_done = one("n1_hi"), one("n1_pool_lo"), one("n1_dve_lo")
        ON_POOL = 3
        WIDE = 4
        with nc.Block() as block:
            @block.sync
            def _(sp):
                def load(b):
                    row0, s = b.at(ROWS), b.slot(4)
                    wait(sp, gathered, b.before(4), 16 * G, apart=turns)
                    sp.dma_start(idx[s][:, :], rows_of(d["sums_idx"], b.at(P), P, 1)).then_inc(idx_ld[s], 16)
                    wait(sp, x1_done, b.before(4), apart=turns)
                    sp.dma_start(flat(x[s]), rows_of(d["x"], row0)).then_inc(ld[s], 16)
                    sp.dma_start(flat(ha[s]), rows_of(d["HA"], row0)).then_inc(ld[s], 16)

                def load_types(b):
                    wait(sp, hT_done, b.before(4), NTYPES, apart=turns)
                    sp.dma_start(nt[b.slot(4)][:, :], d["nt_flat"][0:1, bass.ds(b.at(ROWS), ROWS)].broadcast_to(
                        [P, ROWS])).then_inc(nt_ld[b.slot(4)], 16)

                def store_x1(b):
                    wait(sp, x1_done, b)
                    sp.dma_start(rows_of(d["out"], b.at(ROWS)), flat(x1[b.slot(4)])).then_inc(x1_st[b.slot(4)], 16)

                staged(sp, (0, load), (1, load_types), (3, store_x1))
                all_landed(sp, x1_st, 16)

            @block.vector
            def _(dve):
                def heads(ap):
                    return ap.rearrange("p g (h c) -> p g h c", h=HEADS)

                def spread(ap):
                    return ap[:, :, :].unsqueeze(3).broadcast_to([P, G, HEADS, C])

                def combine(b):
                    t, two = t0[b.slot(4)], b.slot(2)
                    den, ws = t[:, :, P:HA], t[:, :, HA:WT]
                    uu = u[two][:, :, :]
                    wait(dve, ld, b, 32)
                    wait(dve, gathered, b, 16 * G)
                    dve.tensor_tensor(tot[two][:, :, :], den, ws, ALU.add).then_inc(small[0], 1)
                    wait(dve, small, b, 4, 1)
                    dve.scalar_tensor_tensor(out=w[two][:, :, :], in0=tot[two][:, :, :], scalar=0.0, in1=ws,
                                             op0=ALU.is_equal, op1=ALU.add).then_inc(small[0], 1)
                    wait(dve, small, b, 4, 2)
                    dve.scalar_tensor_tensor(out=dn[two][:, :, :], in0=w[two][:, :, :], scalar=1e-16, in1=den,
                                             op0=ALU.add, op1=ALU.add).then_inc(small[0], 1)
                    dve.tensor_tensor(heads(uu), heads(ha[b.slot(4)][:, :, 0:P]), spread(w[two]), ALU.mult).then_inc(wide[0], 1)
                    wait(dve, small, b, 4, 3)
                    dve.reciprocal(r[two][:, :, :], dn[two][:, :, :]).then_inc(small[0], 1)
                    wait(dve, wide, b, WIDE, 1)
                    dve.tensor_tensor(uu, uu, t[:, :, 0:P], ALU.add).then_inc(wide[0], 1)
                    wait(dve, wide, b, WIDE, 2)
                    wait(dve, small, b, 4, 4)
                    dve.tensor_tensor(heads(uu), heads(uu), spread(r[two]), ALU.mult).then_inc(wide[0], 1)
                    wait(dve, wide, b, WIDE, 3)
                    dve.tensor_tensor(uu, uu, keep["bias"][:, :].unsqueeze(1).broadcast_to([P, G, P]),
                                      ALU.add).then_inc(wide[0], 1)

                def residual(b):
                    two, four = b.slot(2), b.slot(4)
                    wait(dve, wide, b, WIDE, 4)
                    wait(dve, below_done, b)
                    dve.scalar_tensor_tensor(out=u[two][:, :, :], in0=u[two][:, :, :], scalar=0.0, in1=x[four][:, :, :],
                                             op0=ALU.max, op1=ALU.add).then_inc(xu_done[0], 1)
                    wait(dve, xu_done, b)
                    wait(dve, exp_done, b)
                    wait(dve, x1_st, b.before(4), 16)
                    wait(dve, h_done, b.before(4), G)
                    dve.scalar_tensor_tensor(out=x1[four][:, :, :], in0=e[two][:, :, :], scalar=-1.0, in1=u[two][:, :, :],
                                             op0=ALU.add, op1=ALU.add).then_inc(x1_done[0], 1)
                    wait(dve, x1_done, b, apart=turns)
                    layer_norm_stats(dve, b, x1[four], stats[four], mv[four], stat_done, mv_done, turns)
                    wait(dve, mv_done, b, G)
                    dve.tensor_scalar(rstd[four][:, 0, :], mv[four][:, :, 1], 1e-5, None, ALU.add).then_inc(var_done[0], 1)
                    dve.tensor_scalar(nmr[four][:, 0, :], mv[four][:, :, 0], -1.0, None, ALU.mult).then_inc(var_done[0], 1)

                def by_type(b):
                    wait(dve, nt_ld, b, 16)
                    wait(dve, t_done, b)
                    wait(dve, pool_lo_done, b.before(2))
                    wait(dve, dve_lo_done, b.before(2))
                    for t in range(NTYPES):
                        dve.scalar_tensor_tensor(out=hTm[b.slot(2)][:, t, :], in0=nt[b.slot(4)][:, :], scalar=float(t),
                                                 in1=psT[b.slot(2)][:, :], op0=ALU.is_equal,
                                                 op1=ALU.mult).then_inc(hT_done[0], 1)

                def split_lo(b):
                    two, four = b.slot(2), b.slot(4)
                    wait(dve, hi_done, b)
                    wait(dve, mm_done, b.before(4), G)
                    dve.tensor_tensor(lo[four][:, ON_POOL:, :], hTm[two][:, ON_POOL:, :], hi[four][:, ON_POOL:, :],
                                      ALU.subtract).then_inc(dve_lo_done[0], 1)
                staged(dve, (0, combine), (1, residual), (3, by_type), (4, split_lo))

            @block.gpsimd
            def _(pool):
                def gather(b):
                    wait(pool, idx_ld, b, 16, apart=turns)
                    wait(pool, x1_done, b.before(4), apart=turns)
                    for g in range(G):
                        pool.indirect_dma_start(t0[b.slot(4)][:, g, :], None, d["T0"][:, :], bass.IndirectOffsetOnAxis(
                            ap=idx[b.slot(4)][:, g:g + 1], axis=0)).then_inc(gathered[b.slot(4)], 16)

                def scale(b):
                    four = b.slot(4)
                    wait(pool, h_done, b.before(4), G, apart=turns)
                    wait(pool, var_done, b, 2, apart=turns)
                    pool.tensor_tensor(rstd[four][:, 1, :], rstd[four][:, 0, :], keep["power"][:, :], ALU.pow).then_inc(rstd_done[0], 1)
                    wait(pool, rstd_done, b, apart=turns)
                    pool.tensor_tensor(nmr[four][:, 1, :], nmr[four][:, 0, :], rstd[four][:, 1, :], ALU.mult).then_inc(nmr_done[0], 1)

                def split_lo(b):
                    two, four = b.slot(2), b.slot(4)
                    wait(pool, hi_done, b, apart=turns)
                    wait(pool, mm_done, b.before(4), G, apart=turns)
                    pool.tensor_tensor(lo[four][:, 0:ON_POOL, :], hTm[two][:, 0:ON_POOL, :], hi[four][:, 0:ON_POOL, :],
                                       ALU.subtract).then_inc(pool_lo_done[0], 1)
                staged(pool, (0, gather), (2, scale), (5, split_lo))

            @block.scalar
            def _(act):
                def exponential(b):
                    wait(act, wide, b, WIDE, 4)
                    wait(act, x1_done, b.before(2))
                    act.activation(e[b.slot(2)][:, :, :], u[b.slot(2)][:, :, :], ACT.Relu, scale=-1.0).then_inc(below_done[0], 1)
                    wait(act, below_done, b)
                    act.activation(e[b.slot(2)][:, :, :], e[b.slot(2)][:, :, :], ACT.Exp, scale=-1.0).then_inc(exp_done[0], 1)

                def normalise(b):
                    wait(act, nmr_done, b)
                    wait(act, t_done, b.before(2))
                    for g in range(G):
                        act.activation(h[b.slot(2)][:, g, :], x1[b.slot(4)][:, g, :], ACT.Relu,
                                       bias=nmr[b.slot(4)][:, 1, g:g + 1],
                                       scale=rstd[b.slot(4)][:, 1, g:g + 1]).then_inc(h_done[0], 1)

                def split_hi(b):
                    wait(act, hT_done, b, NTYPES)
                    wait(act, mm_done, b.before(4), G)
                    act.activation(hi[b.slot(4)][:, :, :], hTm[b.slot(2)][:, :, :], ACT.Copy).then_inc(hi_done[0], 1)

                def products(b):
                    wait(act, qkv_st, b.before(4), 32)
                    for g in range(G):
                        wait(act, mm_done, b, G, g + 1)
                        act.activation(qkv[b.slot(4)][:, g, :], psQ[g][:, 0:3 * P], ACT.Copy).then_inc(qkv_done[0], 1)
                    wait(act, qkv_done, b, G)
                    act.dma_start(parts_of(d["QT"], b.at(ROWS)), qkv[b.slot(4)][:, :, 0:P]).then_inc(qkv_st[b.slot(4)], 16)
                    act.dma_start(parts_of(d["KV"], b.at(ROWS)), qkv[b.slot(4)][:, :, P:3 * P]).then_inc(qkv_st[b.slot(4)], 16)
                staged(act, (0, exponential), (2, normalise), (4, split_hi), (5, products))
                all_landed(act, qkv_st, 32)

            @block.tensor
            def _(pe):
                def turn(b):
                    wait(pe, hT_done, b.before(2), NTYPES)
                    for g in range(G):
                        wait(pe, h_done, b, G, g + 1)
                        mm = pe.transpose(psT[b.slot(2)][:, g * P:(g + 1) * P], h[b.slot(2)][:, g, :], ident[:, :])
                    mm.then_inc(t_done[0], 1)

                def project(b):
                    wait(pe, pool_lo_done, b)
                    wait(pe, dve_lo_done, b)
                    for g in range(G):
                        wait(pe, qkv_done, b.before(1), G, g + 1)
                        for t in range(NTYPES):
                            for n, (part, w) in enumerate(((hi, "WN_hi"), (hi, "WN_lo"), (lo, "WN_hi"))):
                                mm = pe.matmul(psQ[g][:, 0:3 * P], part[b.slot(4)][:, t, g * P:(g + 1) * P], keep[w][:, t, :],
                                               start=(t == 0 and n == 0), stop=(t == NTYPES - 1 and n == 2))
                        mm.then_inc(mm_done[0], 1)
                staged(pe, (0, turn), (2, project))


def gather_scores_1(nc, one, ring, ident, d, keep):
    SC = keep["SC1"]
    with ExitStack() as ctx:
        def sb(n, name, shape, dt=F32):
            return [ctx.enter_context(nc.sbuf_tensor(f"a1_{name}{s}", shape, dt)) for s in range(n)]

        idx, kv, q, et = (sb(4, "idx", [P, 2 * G], U32), sb(4, "kv", [P, G, 2 * P]), sb(4, "q", [P, G, P]),
                          sb(4, "et", [P, ROWS], I32))
        kTm, prod = sb(2, "kTm", [P, ETYPES, ROWS]), sb(2, "prod", [P, G, P])
        psT = [ctx.enter_context(nc.psum_tensor(f"a1_psT{s}", [P, ROWS], F32)) for s in range(2)]
        psK = [ctx.enter_context(nc.psum_tensor(f"a1_psK{s}", [P, G, P], F32)) for s in range(2)]
        idx_ld, et_ld, gathered, v_st = ring("a1_idx_ld", 4), ring("a1_et_ld", 4), ring("a1_gathered", 4), ring("a1_v_st", 4)
        t_done, kT_done, mm_done, prod_done, sc_done = one("a1_t"), one("a1_kT"), one("a1_mm"), one("a1_prod"), one("a1_sc")
        turns = one("a1_turns")[0]
        with nc.Block() as block:
            @block.sync
            def _(sp):
                def load(b):
                    wait(sp, gathered, b.before(4), 16 * 2 * G)
                    sp.dma_start(idx[b.slot(4)][:, :], rows_of(d["edge_idx"], b.at(P), P, 1)).then_inc(idx_ld[b.slot(4)], 16)
                    wait(sp, kT_done, b.before(4), ETYPES)
                    sp.dma_start(et[b.slot(4)][:, :], d["et_flat"][0:1, bass.ds(b.at(ROWS), ROWS)].broadcast_to(
                        [P, ROWS])).then_inc(et_ld[b.slot(4)], 16)
                staged(sp, (0, load))

            @block.scalar
            def _(act):
                def store(b):
                    wait(act, gathered, b, 16 * 2 * G)
                    act.dma_start(parts_of(d["M"], b.at(ROWS)), kv[b.slot(4)][:, :, P:2 * P]).then_inc(v_st[b.slot(4)], 16)
                staged(act, (0, store))
                all_landed(act, v_st, 16)

            @block.gpsimd
            def _(pool):
                def gather(b):
                    i = idx[b.slot(4)]
                    wait(pool, idx_ld, b, 16, apart=turns)
                    wait(pool, v_st, b.before(4), 16, apart=turns)
                    wait(pool, t_done, b.before(4), apart=turns)
                    wait(pool, prod_done, b.before(4), apart=turns)
                    for g in range(G):
                        pool.indirect_dma_start(kv[b.slot(4)][:, g, :], None, d["KV"][:, :], bass.IndirectOffsetOnAxis(
                            ap=i[:, g:g + 1], axis=0)).then_inc(gathered[b.slot(4)], 16)
                        pool.indirect_dma_start(q[b.slot(4)][:, g, :], None, d["QT"][:, :], bass.IndirectOffsetOnAxis(
                            ap=i[:, G + g:G + g + 1], axis=0)).then_inc(gathered[b.slot(4)], 16)
                staged(pool, (0, gather))

            @block.tensor
            def _(pe):
                def turn(b):
                    wait(pe, gathered, b, 16 * 2 * G)
                    wait(pe, kT_done, b.before(2), ETYPES)
                    for g in range(G):
                        mm = pe.transpose(psT[b.slot(2)][:, g * P:(g + 1) * P], kv[b.slot(4)][:, g, 0:P], ident[:, :])
                    mm.then_inc(t_done[0], 1)

                def through_edges(b):
                    wait(pe, prod_done, b.before(2))
                    wait(pe, kT_done, b, ETYPES)
                    for g in range(G):
                        for t in range(ETYPES):
                            mm = pe.matmul(psK[b.slot(2)][:, g, :], kTm[b.slot(2)][:, t, g * P:(g + 1) * P],
                                           keep["WE"][:, t, :], start=(t == 0), stop=(t == ETYPES - 1))
                    mm.then_inc(mm_done[0], 1)
                staged(pe, (0, turn), (1, through_edges))

            @block.vector
            def _(dve):
                def by_type(b):
                    wait(dve, t_done, b)
                    wait(dve, et_ld, b, 16)
                    wait(dve, mm_done, b.before(2))
                    for t in range(ETYPES):
                        dve.scalar_tensor_tensor(out=kTm[b.slot(2)][:, t, :], in0=et[b.slot(4)][:, :], scalar=float(t),
                                                 in1=psT[b.slot(2)][:, :], op0=ALU.is_equal,
                                                 op1=ALU.mult).then_inc(kT_done[0], 1)

                def score(b):
                    wait(dve, mm_done, b)
                    wait(dve, sc_done, b.before(2))
                    dve.tensor_tensor(prod[b.slot(2)][:, :, :], q[b.slot(4)][:, :, :], psK[b.slot(2)][:, :, :],
                                      ALU.mult).then_inc(prod_done[0], 1)
                    wait(dve, prod_done, b)
                    dve.tensor_reduce(SC[:, 0, bass.ds(b.at(G), G)], prod[b.slot(2)][:, :, :], AX.X,
                                      ALU.add).then_inc(sc_done[0], 1)
                staged(dve, (0, by_type), (1, score))


def gnn(nc, d):
    for name, shape in (("HA", (NP, P + HEADS)), ("E0", (NP, 2 * HEADS)), ("M", (NP, P)), ("T0", (NP + 1, P + 2 * HEADS)),
                        ("QT", (NP, P)), ("KV", (NP, 2 * P)), ("brow", (NT, P))):
        d[name] = nc.dram_tensor(f"scratch_{name}", shape, F32, kind="Internal").ap()
    for name in ("first_idx", "sums_idx"):
        d[name] = nc.dram_tensor(f"scratch_{name}", (NB * P, G), U32, kind="Internal").ap()
    d["brow_flat"] = d["brow"].rearrange("(o t) e -> o (t e)", o=1)
    with ExitStack() as ctx:
        def sb(name, shape, dt=F32):
            return ctx.enter_context(nc.sbuf_tensor(name, shape, dt))

        held = []

        def sem(name):
            held.append(nc.alloc_semaphore(name=name))
            return held[-1]

        def one(name):
            return [sem(name)]

        def ring(name, n):
            return [sem(f"{name}_{i}") for i in range(n)]

        def phase_ends():
            nc.clear_and_free_semaphores(held)
            nc.all_engine_barrier()
            held.clear()

        ident = sb("ident", [P, P])
        keep = {
            "WX": sb("WX", [P, P + 2 * HEADS]), "WE": sb("WE", [P, ETYPES, P]),
            "WN_hi": sb("WN_hi", [P, NTYPES, 3 * P], F32R), "WN_lo": sb("WN_lo", [P, NTYPES, 3 * P], F32R),
            "bias": sb("bias", [P, P]), "power": sb("power", [P, G]),
            "sidx": sb("sidx", [P, NT], U32), "SC": sb("SC", [P, HEADS, NT]), "SE": sb("SE", [P, HEADS, NT]),
            "SC1": sb("SC1", [P, 1, NT]),
        }
        prepare(nc, sem, ident, d, keep)
        phase_ends()
        count_edges(nc, one, d)
        phase_ends()
        project_nodes(nc, one, ring, ident, d, keep)
        phase_ends()
        gather_scores_0(nc, one, ring, d, keep)
        phase_ends()
        segment_softmax(nc, sem, ident, d, HEADS, keep["SC"], keep["SE"], None, "s0")
        phase_ends()
        segment_sums(nc, one, ring, d, keep, HEADS, keep["SC"], keep["SE"], d["T0"], "b0")
        phase_ends()
        finish_0_project_1(nc, one, ring, ident, d, keep)
        phase_ends()
        gather_scores_1(nc, one, ring, ident, d, keep)
        phase_ends()
        segment_softmax(nc, sem, ident, d, 1, keep["SC1"], None, -1.0e9, "s1")
        phase_ends()
        segment_sums(nc, one, ring, d, keep, 1, keep["SC1"], None, d["out"], "b1")
        phase_ends()


def kernel(x, src, dst, edge_type_8, node_type_4, L0_gnn_W, L0_gnn_att_src, L0_gnn_att_dst, L0_gnn_bias,
           L1_gnn_W_Q, L1_gnn_W_K, L1_gnn_W_V, L1_gnn_W_edge, L1_gnn_mu):
    import numpy as np
    import concourse.bacc as bacc
    from concourse.bass_utils import run_bass_kernel_spmd

    def padded(a, fill):
        a = np.asarray(a)
        return np.concatenate([a, np.full((NP - N,) + a.shape[1:], fill, a.dtype)])

    src_p, dst_p = padded(src, 0), padded(dst, N)
    before = np.concatenate([np.full(1, N + 2, dst_p.dtype), dst_p[:-1]])
    behind = np.concatenate([dst_p[1:], np.full(1, N + 1, dst_p.dtype)])
    tiles, tiles_before, tiles_behind = (a.reshape(NT, P) for a in (dst_p, before, behind))
    arrays = {
        "x": padded(x, 0.0),
        "edge_idx": np.concatenate([a.reshape(NB, G, P).transpose(0, 2, 1) for a in (src_p, dst_p)],
                                   axis=2).reshape(NB * P, 2 * G).astype(src_p.dtype),
        "dst_cols": np.stack([tiles.T, tiles_before.T]),
        "dst_rows": np.concatenate([tiles_before[:, :1], tiles, tiles_behind[:, -1:]], axis=1),
        "dst_ends": np.stack([np.concatenate([before[:1], tiles[:, -1]]), np.concatenate([tiles[:, 0], behind[-1:]])]),
        "dst_flat": dst_p.reshape(1, NP),
        "et_flat": padded(edge_type_8, 0).reshape(1, NP),
        "nt_flat": padded(node_type_4, 0).reshape(NB, P, G).transpose(0, 2, 1).reshape(1, NP),
        "W": L0_gnn_W, "att_src": np.asarray(L0_gnn_att_src).reshape(1, P),
        "att_dst": np.asarray(L0_gnn_att_dst).reshape(1, P), "bias": np.asarray(L0_gnn_bias).reshape(1, P),
        "W_Q": L1_gnn_W_Q, "W_K": L1_gnn_W_K, "W_V": L1_gnn_W_V, "W_edge": L1_gnn_W_edge,
        "mu": np.asarray(L1_gnn_mu).reshape(1, ETYPES),
    }
    nc = bacc.Bacc("TRN2", target_bir_lowering=False, num_devices=1)
    given, d = {}, {}
    for name, a in arrays.items():
        a = np.ascontiguousarray(a)
        given[f"in_{name}"] = a
        dt = U32 if name == "edge_idx" else mybir.dt.from_np(a.dtype)
        d[name] = nc.dram_tensor(f"in_{name}", a.shape, dt, kind="ExternalInput").ap()
    d["out"] = nc.dram_tensor("out_0", (NP + SPARE, P), F32, kind="ExternalOutput").ap()
    gnn(nc, d)
    r = run_bass_kernel_spmd(nc, [given], core_ids=[0])
    return r.results[0]["out_0"][:N]
```
